# Optimizing a Trainium2 kernel written in Bass

```python
import numpy as np
import jax
import jax.numpy as jnp

def _softmax(x, axis=-1):
    return jax.nn.softmax(x, axis=axis)

def _gelu(x):
    return jax.nn.gelu(x, approximate=True)

def _silu(x):
    return jax.nn.silu(x)

def _sigmoid(x):
    return jax.nn.sigmoid(x)

def _layernorm(x, axis=-1, eps=1e-05):
    m = jnp.mean(x, axis=axis, keepdims=True)
    v = jnp.var(x, axis=axis, keepdims=True)
    return (x - m) / jnp.sqrt(v + eps)

def _scatter_add(tgt, idx, src, axis=0):
    return tgt.at[idx].add(src)

def _segment_sum(src, seg, n):
    return jax.ops.segment_sum(src, seg, n)
kernel_name = 'mk_gnn_preln_d4_gnn_r8_8fc7ff'

def setup_inputs(seed: int=0):
    np.random.seed(seed)
    _w = jnp.asarray

    def _rec_inputs():
        import jax
        import jax.numpy as jnp
        _gk = jax.random.key(seed)
        x = -0.0001006 + 1 * jax.random.normal(jax.random.fold_in(_gk, 1), (12500, 48), jnp.float32)
        src = jax.random.randint(jax.random.fold_in(_gk, 2), (400000,), 0, 12500, jnp.int32)
        dst = jnp.minimum((12500 * jax.random.uniform(jax.random.fold_in(_gk, 3), (400000,)) ** 2.0).astype(jnp.int32), 99999)
        _o = jnp.argsort(dst, stable=True)
        src = src[_o]
        dst = dst[_o]
        edge_attr_40 = jax.random.uniform(jax.random.fold_in(_gk, 13), (400000, 40), jnp.float32, 0.0, 1)
        edge_weight = jax.random.uniform(jax.random.fold_in(_gk, 15), (400000,), jnp.float32, 0.0, 0.999998)
        node_type_119 = jax.random.randint(jax.random.fold_in(_gk, 16), (12500,), 0, 119, jnp.int32)
        node_vec = jax.random.uniform(jax.random.fold_in(_gk, 17), (12500,), jnp.float32, 0.0, 1.49999)
        return (x, src, dst, edge_attr_40, edge_weight, node_type_119, node_vec)
    x, src, dst, edge_attr_40, edge_weight, node_type_119, node_vec = _rec_inputs()

    def _L0_gnn_setup():
        import jax, jax.numpy as jnp
        import numpy as np
        N_NODES = 12500
        N_EDGES = 200000
        D_IN = 48
        D_OUT = 48
        key = jax.random.key(seed)
        k1, k2, k3, k4, k5 = jax.random.split(key, 5)
        x = jax.random.normal(k1, (N_NODES, D_IN), dtype=jnp.float32)
        init_range = np.sqrt(6.0 / (D_IN + D_OUT)).astype(np.float32)
        w = jax.random.uniform(k2, (D_IN, D_OUT), dtype=jnp.float32, minval=-init_range, maxval=init_range)
        b = jnp.zeros((D_OUT,), dtype=jnp.float32)
        edge_src = jax.random.randint(k3, (N_EDGES,), 0, N_NODES, dtype=jnp.int32)
        edge_dst = jax.random.randint(k4, (N_EDGES,), 0, N_NODES, dtype=jnp.int32)
        adj_vals = jax.random.uniform(k5, (N_EDGES,), dtype=jnp.float32)
        return {'x': x, 'w': w, 'b': b, 'edge_src': edge_src, 'edge_dst': edge_dst, 'adj_vals': adj_vals}
    _L0_gnn_all = _L0_gnn_setup()
    _L0_gnn_in = {k: v for k, v in _L0_gnn_all.items() if k in ('w', 'b')}
    del _L0_gnn_all

    def _L1_gnn_setup():
        import jax, jax.numpy as jnp
        import numpy as np
        CUTOFF = 6.0
        LN_EPS = 1e-05
        key = jax.random.key(seed)
        ks = jax.random.split(key, 16)
        N, E, H, R, NEL, G = (6250, 100000, 48, 40, 119, 32)
        inp = {'h': jax.random.normal(ks[0], (N, H), jnp.float32), 'edge_index': jax.random.randint(ks[1], (2, E), 0, N, jnp.int64), 'edge_attr': jax.random.uniform(ks[2], (E, R), jnp.float32), 'distances': jax.random.uniform(ks[3], (E,), jnp.float32) * 7.0, 'atom_z': jax.random.randint(ks[4], (N,), 0, NEL, jnp.int64), 'node_mult': jax.random.uniform(ks[5], (N,), jnp.float32) + 0.5, 'batch': jnp.zeros((N,), jnp.int64), 'W1': jax.random.normal(ks[6], (H, R), jnp.float32) / np.sqrt(R), 'b1': jax.random.normal(ks[7], (H,), jnp.float32) * 0.01, 'W2': jax.random.normal(ks[8], (H, H), jnp.float32) / np.sqrt(H), 'b2': jax.random.normal(ks[9], (H,), jnp.float32) * 0.01, 'emb': jax.random.normal(ks[10], (NEL, G), jnp.float32) * 0.01, 'adaptW': jax.random.normal(ks[11], (G, G), jnp.float32) * 0.01, 'gamma': jnp.ones((H,), jnp.float32), 'beta': jnp.zeros((H,), jnp.float32)}
        return inp
    _L1_gnn_all = _L1_gnn_setup()
    _L1_gnn_in = {k: v for k, v in _L1_gnn_all.items() if k in ('W1', 'b1', 'W2', 'b2', 'emb', 'adaptW', 'gamma', 'beta')}
    del _L1_gnn_all

    def _L2_gnn_setup():
        import jax, jax.numpy as jnp
        import numpy as np
        NUM_LAYERS = 2
        N_NODES = 12500
        N_EDGES = 200000
        D_FEAT = 48

        def spmm(edge_index, edge_weight, x, n):
            src, dst = (edge_index[0], edge_index[1])
            msgs = x[src] * edge_weight[:, None]
            return jax.ops.segment_sum(msgs, dst, num_segments=n)
        key = jax.random.key(seed)
        k1, k2, k3 = jax.random.split(key, 3)
        features = jax.random.normal(k1, (N_NODES, D_FEAT), dtype=jnp.float32)
        edge_weight = jax.random.uniform(k2, (N_EDGES,), dtype=jnp.float32)
        edge_index = jax.random.randint(k3, (2, N_EDGES), 0, N_NODES, dtype=jnp.int64)
        return {'features': features, 'edge_weight': edge_weight, 'edge_index': edge_index}
    _L2_gnn_all = _L2_gnn_setup()
    _L2_gnn_in = {k: v for k, v in _L2_gnn_all.items() if k in ()}
    del _L2_gnn_all

    def _L3_gnn_setup():
        import jax, jax.numpy as jnp
        import numpy as np
        N_NODES = 6250
        N_EDGES = 200000
        D_IN = 48
        D_OUT = 48
        K = 4
        key = jax.random.key(seed)
        k1, k2, k3, k4, k5 = jax.random.split(key, 5)
        x = jax.random.normal(k1, (N_NODES, D_IN), dtype=jnp.float32)
        edge_index = jax.random.randint(k2, (2, N_EDGES), 0, N_NODES, dtype=jnp.int64)
        weight = jax.random.normal(k3, (K, D_IN, D_OUT), dtype=jnp.float32) * (1.0 / np.sqrt(D_IN))
        bias = jax.random.normal(k4, (D_OUT,), dtype=jnp.float32) * 0.01
        return {'x': x, 'edge_index': edge_index, 'weight': weight, 'bias': bias}
    _L3_gnn_all = _L3_gnn_setup()
    _L3_gnn_in = {k: v for k, v in _L3_gnn_all.items() if k in ('weight', 'bias')}
    del _L3_gnn_all
    return {'x': x, 'src': src, 'dst': dst, 'edge_attr_40': edge_attr_40, 'edge_weight': edge_weight, 'node_type_119': node_type_119, 'node_vec': node_vec, 'L0_gnn_w': _L0_gnn_in['w'], 'L0_gnn_b': _L0_gnn_in['b'], 'L1_gnn_W1': _L1_gnn_in['W1'], 'L1_gnn_b1': _L1_gnn_in['b1'], 'L1_gnn_W2': _L1_gnn_in['W2'], 'L1_gnn_b2': _L1_gnn_in['b2'], 'L1_gnn_emb': _L1_gnn_in['emb'], 'L1_gnn_adaptW': _L1_gnn_in['adaptW'], 'L1_gnn_gamma': _L1_gnn_in['gamma'], 'L1_gnn_beta': _L1_gnn_in['beta'], 'L3_gnn_weight': _L3_gnn_in['weight'], 'L3_gnn_bias': _L3_gnn_in['bias']}

def reference(x, src, dst, edge_attr_40, edge_weight, node_type_119, node_vec, L0_gnn_w, L0_gnn_b, L1_gnn_W1, L1_gnn_b1, L1_gnn_W2, L1_gnn_b2, L1_gnn_emb, L1_gnn_adaptW, L1_gnn_gamma, L1_gnn_beta, L3_gnn_weight, L3_gnn_bias):
    import jax
    import jax.numpy as jnp

    def _L0_gnn_ref(x, w, b, edge_src, edge_dst, adj_vals):
        import jax, jax.numpy as jnp
        import numpy as np
        N_NODES = 12500
        N_EDGES = 200000
        D_IN = 48
        D_OUT = 48
        xw = jnp.matmul(x, w)
        msgs = adj_vals[:, None] * xw[edge_src]
        agg = jax.ops.segment_sum(msgs, edge_dst, num_segments=N_NODES)
        return jax.nn.relu(agg + b)

    def _L1_gnn_ref(h, edge_index, edge_attr, distances, atom_z, node_mult, batch, W1, b1, W2, b2, emb, adaptW, gamma, beta):
        import jax, jax.numpy as jnp
        import numpy as np
        CUTOFF = 6.0
        LN_EPS = 1e-05
        src, dst = (edge_index[0], edge_index[1])
        N = h.shape[0]
        gate = jax.nn.silu(edge_attr @ W1.T + b1) @ W2.T + b2
        ei = emb[atom_z[src]]
        ej = emb[atom_z[dst]]
        adapt_logit = jnp.sum(ei * (ej @ adaptW.T), axis=-1, keepdims=True)
        gate = gate + adapt_logit
        cw = jnp.where(distances < CUTOFF, 0.5 * (jnp.cos(jnp.pi * distances / CUTOFF) + 1.0), 0.0)
        mj = node_mult[dst]
        msg = gate * h[dst] * (cw * mj)[:, None]
        agg = jax.ops.segment_sum(msg, src, num_segments=N)
        tot = jax.ops.segment_sum(mj, src, num_segments=N)
        agg = agg / jnp.clip(tot, 1e-08, None)[:, None]
        x = h + agg
        mu = jnp.mean(x, axis=-1, keepdims=True)
        var = jnp.mean(jnp.square(x - mu), axis=-1, keepdims=True)
        return (x - mu) / jnp.sqrt(var + LN_EPS) * gamma + beta

    def _L2_gnn_ref(features, edge_weight, edge_index):
        import jax, jax.numpy as jnp
        import numpy as np
        NUM_LAYERS = 2
        N_NODES = 12500
        N_EDGES = 200000
        D_FEAT = 48

        def spmm(edge_index, edge_weight, x, n):
            src, dst = (edge_index[0], edge_index[1])
            msgs = x[src] * edge_weight[:, None]
            return jax.ops.segment_sum(msgs, dst, num_segments=n)
        n = features.shape[0]
        scale = 1.0 / (NUM_LAYERS + 1)
        avg = features * scale
        x = features
        for _ in range(NUM_LAYERS):
            x = spmm(edge_index, edge_weight, x, n)
            avg = avg + x * scale
        return avg

    def _L3_gnn_ref(x, edge_index, weight, bias):
        import jax, jax.numpy as jnp
        import numpy as np
        N_NODES = 6250
        N_EDGES = 200000
        D_IN = 48
        D_OUT = 48
        K = 4
        'PyG ChebConv forward with sym normalization, lambda_max=2.0.\n\n            L_hat = 2L/lambda_max - I. With lambda_max=2 and sym Laplacian, the\n            diagonal becomes 0 and off-diagonal weights are -d_i^{-1/2} d_j^{-1/2}.\n            T0 = x, T1 = L_hat x, Tk = 2 L_hat T_{k-1} - T_{k-2};  out = sum_k Tk W_k + b.\n            '
        n = x.shape[0]
        row, col = (edge_index[0], edge_index[1])
        ew = (row != col).astype(x.dtype)
        deg = jax.ops.segment_sum(ew, row, num_segments=n)
        dis = jnp.where(deg > 0, jax.lax.rsqrt(deg), 0.0)
        w = -dis[row] * ew * dis[col]

        def prop(h):
            return jax.ops.segment_sum(w[:, None] * h[row], col, num_segments=n)
        tx0 = x
        out = tx0 @ weight[0]
        tx1 = prop(x)
        out = out + tx1 @ weight[1]
        for k in range(2, weight.shape[0]):
            tx2 = 2.0 * prop(tx1) - tx0
            out = out + tx2 @ weight[k]
            tx0, tx1 = (tx1, tx2)
        return out + bias
    edge_index = jnp.stack([src, dst])
    batch0 = jnp.zeros((12500,), jnp.int32)
    h = jnp.maximum(_layernorm(x, axis=-1), 0.0)
    x = x + _L0_gnn_ref(h, L0_gnn_w, L0_gnn_b, src, dst, edge_weight)
    h = jnp.maximum(_layernorm(x, axis=-1), 0.0)
    x = x + _L1_gnn_ref(h, edge_index, edge_attr_40, edge_weight, node_type_119, node_vec, batch0, L1_gnn_W1, L1_gnn_b1, L1_gnn_W2, L1_gnn_b2, L1_gnn_emb, L1_gnn_adaptW, L1_gnn_gamma, L1_gnn_beta)
    h = jnp.maximum(_layernorm(x, axis=-1), 0.0)
    x = x + _L2_gnn_ref(h, edge_weight, edge_index)
    h = jnp.maximum(_layernorm(x, axis=-1), 0.0)
    x = x + _L3_gnn_ref(h, edge_index, L3_gnn_weight, L3_gnn_bias)
    return x

_drawn_inputs = setup_inputs


def setup_inputs(seed=0):
    import zlib

    import numpy as np

    out = dict(_drawn_inputs(seed))
    spreads = {'L0_gnn_b': (0.0, 0.319), 'L1_gnn_gamma': (1.0, 0.2), 'L1_gnn_beta': (0.0, 0.544)}
    factors = {'edge_attr_40': 8.0,
     'node_vec': 8.0,
     'L1_gnn_b1': 8.0,
     'L1_gnn_b2': 8.0,
     'L1_gnn_emb': 8.0,
     'L1_gnn_adaptW': 8.0,
     'L3_gnn_bias': 8.0}
    for name, (base, spread) in spreads.items():
        noise = np.random.default_rng([zlib.crc32(name.encode()), seed]).standard_normal(out[name].shape)
        drawn = base * np.exp(spread * noise) if base else spread * noise
        out[name] = jnp.asarray(drawn.astype(out[name].dtype))
    for name, factor in factors.items():
        out[name] = (out[name] * factor).astype(out[name].dtype)
    return out
```

```python
from contextlib import ExitStack
from math import pi

import concourse.bass as bass
from concourse import mybir

F32, I32, BF16 = mybir.dt.float32, mybir.dt.int32, mybir.dt.bfloat16
ALU, ACT, AX = mybir.AluOpType, mybir.ActivationFunctionType, mybir.AxisListType
DVE_ENGINE, PE_ENGINE = mybir.EngineType.DVE, mybir.EngineType.PE

P = 128
RING = 5
K = 5
U = RING * K

EW, DREL, IDX, EW3, SWIN, SREL, DWIN, CW = range(8)
NF = 8
CUTOFF = 6.0
LN_EPS = 1e-5
OUT_OF_BOUNDS = 4.0e6


def ceil_div(a, b):
    return -(-a // b)


class Chain:

    def __init__(self, engine, sem, start=0):
        self.engine, self.sem, self.n = engine, sem, start

    def __call__(self, ins):
        ins.then_inc(self.sem, 1)
        self.n += 1
        return self

    def done(self):
        self.engine.wait_ge(self.sem, self.n)

    def step(self, ins):
        self(ins)
        self.done()


def lone_wait(engine, sem, value):
    engine.wait_ge(sem, value)
    engine.nop(nofuse=True)


def turns(engine, n, body):
    body(0, True)
    with engine.Fori(1, n) as i:
        body(i, False)


def gnn_kernel(nc, x, src, dst, edge_attr, edge_weight, node_type, node_vec, w0, b0, w1, b1, w2, b2,
               emb, adapt, gamma, beta, cheb, cheb_bias, out):
    N, D = x.shape
    E, R = edge_attr.shape
    NT, G = emb.shape
    NCHEB = cheb.shape[0]
    W = ceil_div(N, P)
    TAIL = N - (W - 1) * P
    EC = E // P
    ET = EC // U
    QC = ceil_div(E + W * (P - 1), P * U) * U
    QT = QC // U
    SB = 4
    SG = ceil_div(ceil_div(E + W * (SB * P - 1), SB * P), RING) * RING
    ST = SG // RING
    SROWS = SG * SB * P
    REC = R + NF
    MSG = D + 4
    TOT, DEG, MREL = D, D + 1, D + 2
    AC = D + 2
    T0 = D + G
    HV = D + G + 1
    assert E == ET * P * U and R + NF == 48 and NF == 8 and W <= P and K * W <= 512

    ctx = ExitStack()

    def scoped(stack, name, shape, dt):
        return stack.enter_context(nc.sbuf_tensor(name, shape, dt))

    def sb(name, shape, dt=F32):
        return scoped(ctx, name, shape, dt)

    def sem(name):
        return ctx.enter_context(nc.semaphore(name))

    def sems(name):
        return [sem(f"{name}{g}") for g in range(RING)]

    rec_dram = nc.dram_tensor("records_by_dst", [QC * P, REC], F32).ap()
    msg_dram = nc.dram_tensor("messages_by_src", [SROWS, MSG], F32).ap()
    u_dram = nc.dram_tensor("src_embedding_of_edges", [P, QC * G], F32).ap()
    tab0_dram = nc.dram_tensor("table_first", [P * W, T0], F32).ap()
    tab_dram = nc.dram_tensor("table", [P * W, D], F32).ap()
    types_dram = nc.dram_tensor("table_types", [NT, 2 * G], F32).ap()

    with ctx:
        win_d = sb("win_d", [1, QC], I32)
        win_s = sb("win_s", [1, SG], I32)
        ident = sb("ident", [P, P])
        iota = sb("iota", [P, P])
        iota_b = sb("iota_b", [P, P], BF16)
        lt_b = sb("lt_b", [P, P], BF16)
        ones_b = sb("ones_b", [P, P], BF16)
        ones_f = sb("ones_f", [P, P])
        w0_sb = sb("w0_sb", [D, D])
        w1t = sb("w1t", [R, D])
        w2t = sb("w2t", [D, D])
        cheb_sb = sb("cheb_sb", [D, NCHEB, D])
        b1_col = sb("b1_col", [D, 1])
        b2_rep = sb("b2_rep", [1, K, D])
        rows = sb("rows", [P, 4, D])
        B0, GAMMA, BETA, BIAS = range(4)
        run_d = sb("run_d", [P, W])
        run_s = sb("run_s", [P, W])
        onehot_w = sb("onehot_w", [P, RING, K, W], BF16)
        rank = sb("rank", [P, K, W])
        mean = sb("mean", [P, W])
        var = sb("var", [P, W])
        mult = sb("mult", [P, W])
        dis = sb("dis", [P, W])
        half_pi = sb("half_pi", [P, 1])
        types_i = sb("types_i", [P, W], I32)

        v = sem("v")
        vn = [0]

        mark = {}

        def chain(engine):
            c = Chain(engine, v, vn[0])
            return c

        def keep(c):
            vn[0] = c.n

        edges = ExitStack()
        emeta = scoped(edges, "emeta", [P, EC, NF], F32)
        with ExitStack() as s0:
            def tmp(name, shape, dt=F32):
                return scoped(s0, name, shape, dt)

            src_i = tmp("src_i", [P, EC], I32)
            dst_i = tmp("dst_i", [P, EC], I32)
            t_i = tmp("t_i", [P, EC], I32)
            wf, wf2 = src_i[:, :].bitcast(F32), dst_i[:, :].bitcast(F32)
            junk_v = t_i[:, :].bitcast(F32)
            pcol = tmp("pcol", [P, 1])
            ge_d = tmp("ge_d", [P, W])
            ge_s = tmp("ge_s", [P, W])
            near = tmp("near", [P, W])
            cnt = tmp("cnt", [P, 2, W + 1])
            cnt_i = tmp("cnt_i", [P, 2, W], I32)
            nb = tmp("nb", [P, 2, W])
            inc = tmp("inc", [P, 2, W])
            begin = tmp("begin", [P, 2, W])
            begin_col = tmp("begin_col", [P, 2])
            sel = tmp("sel", [P, W])
            cols = tmp("cols", [P, 512])
            started = tmp("started", [P, 512], BF16)
            w_rows = tmp("w_rows", [D, 2, D])
            emb_sb = tmp("emb_sb", [P, G])
            adapt_sb = tmp("adapt_sb", [G, G])
            adapt_t = tmp("adapt_t", [G, G])
            emb_t = tmp("emb_t", [G, P])
            two = tmp("two", [P, 2 * G])
            types_w = tmp("types_w", [P, P], I32)
            nodes_w = tmp("nodes_w", [P, 2, P])
            fill = tmp("fill", [P, 25, REC])

            s_in, s_edge, s_fill, s_out = (sem(f"s0_{n}") for n in ("in", "edge", "fill", "out"))
            s_iota, s_pe, s_act, s_hist, s_uv, s_ready, s_ge = (
                sem(f"s0_{n}") for n in ("iota", "pe", "act", "hist", "uv", "ready", "ge"))
            ps = [s0.enter_context(nc.psum_tensor(f"ps0_{b}", [P, 512], F32)) for b in range(8)]
            NIN = 11 + 4 + K

            NIN = 11 + 4 + K
            full = (W - 1) * P
            with nc.Block() as block:
                @block.vector
                def _(dve):
                    c = chain(dve)
                    c(dve.memset(fill[:, :, :], 0.0))
                    c(dve.memset(types_w[:, :], 0))
                    c(dve.memset(nodes_w[:, :, :], 0.0))
                    c(dve.memset(emb_sb[:, :], 0.0))
                    c(dve.memset(w_rows[:, :, :], 0.0))
                    c(dve.memset(half_pi[:, :], pi / 2))
                    c(dve.memset(ones_b[:, :], 1.0))
                    c(dve.memset(ones_f[:, :], 1.0))
                    c(dve.memset(cnt[:, :, :], 0.0))
                    mark["zeroed"] = c.n
                    c.done()
                    for f in (DREL, SWIN, SREL):
                        c(dve.memset(fill[:, :, R + f:R + f + 1], -1.0))
                    mark["fill"] = c.n
                    dve.wait_ge(s_iota, 3)
                    c(dve.tensor_copy(iota_b[:, :], iota[:, :]))
                    c(dve.tensor_scalar(ident[:, :], iota[:, :], pcol[:, :], None, ALU.is_equal))
                    c(dve.tensor_scalar(lt_b[:, :], iota[:, :], pcol[:, :], None, ALU.is_gt))
                    c(dve.tensor_scalar(near[:, :], iota[:, 0:W], -1.0, 0.5, ALU.mult, ALU.add))
                    dve.wait_ge(s_edge, 32)
                    c(dve.tensor_tensor(emeta[:, :, EW3], src_i[:, :], dst_i[:, :], ALU.not_equal))
                    c.step(dve.tensor_scalar(t_i[:, :], src_i[:, :], P - 1, None, ALU.bitwise_and))
                    c.step(dve.tensor_copy(emeta[:, :, SREL], t_i[:, :]))
                    c.step(dve.tensor_scalar(t_i[:, :], src_i[:, :], 7, None, ALU.logical_shift_right))
                    c.step(dve.tensor_copy(emeta[:, :, SWIN], t_i[:, :]))
                    c.step(dve.scalar_tensor_tensor(out=emeta[:, :, IDX], in0=emeta[:, :, SREL], scalar=float(W),
                                                    in1=emeta[:, :, SWIN], op0=ALU.mult, op1=ALU.add))
                    c.step(dve.tensor_scalar(t_i[:, :], dst_i[:, :], P - 1, None, ALU.bitwise_and))
                    c.step(dve.tensor_copy(emeta[:, :, DREL], t_i[:, :]))
                    c.step(dve.tensor_scalar(t_i[:, :], dst_i[:, :], 7, None, ALU.logical_shift_right))
                    c.step(dve.tensor_copy(emeta[:, :, DWIN], t_i[:, :]))
                    mark["src used"] = c.n
                    dve.wait_ge(s_edge, 48)
                    c(dve.tensor_copy(emeta[:, :, EW], wf))
                    c.step(dve.tensor_scalar(t_i[:, :], wf, 0.5 / CUTOFF, None, ALU.mult))
                    c.step(dve.tensor_copy(wf2, t_i[:, :]))
                    c.step(dve.scalar_tensor_tensor(out=wf2, in0=wf2, scalar=-2 * CUTOFF, in1=wf,
                                                    op0=ALU.mult, op1=ALU.add))
                    c.step(dve.scalar_tensor_tensor(out=wf2, in0=wf2, scalar=-1.0, in1=wf2,
                                                    op0=ALU.mult, op1=ALU.max))
                    mark["remainder"] = c.n
                    dve.wait_ge(s_pe, 1)
                    c.step(dve.tensor_scalar(emeta[:, :, CW], emeta[:, :, CW], 0.5, 0.5, ALU.mult, ALU.add))
                    c.step(dve.scalar_tensor_tensor(out=emeta[:, :, CW], in0=wf, scalar=CUTOFF,
                                                    in1=emeta[:, :, CW], op0=ALU.is_lt, op1=ALU.mult))
                    keep(c)

                @block.sync
                def _(sp):
                    sp.dma_start(src_i[:, :], src.rearrange("(p n) -> p n", p=P)).then_inc(s_edge, 16)
                    sp.dma_start(dst_i[:, :], dst.rearrange("(p n) -> p n", p=P)).then_inc(s_edge, 16)
                    sp.wait_ge(v, mark["zeroed"])
                    loads = [
                        (types_w[0:W - 1, :], node_type[0:full].rearrange("(w p) -> w p", p=P)),
                        (types_w[W - 1:W, 0:TAIL], node_type[full:N].rearrange("(w p) -> w p", w=1)),
                        (nodes_w[0:W - 1, 1, :], node_vec[0:full].rearrange("(w p) -> w p", p=P)),
                        (nodes_w[W - 1:W, 1, 0:TAIL], node_vec[full:N].rearrange("(w p) -> w p", w=1)),
                        (w0_sb[:, :], w0), (w_rows[:, 0, 0:R], w1), (w_rows[:, 1, :], w2),
                        (cheb_sb[:, :, :], cheb.rearrange("k i o -> i k o")),
                        (b1_col[:, :], b1.rearrange("(p a) -> p a", a=1)),
                        (emb_sb[0:NT, :], emb), (adapt_sb[:, :], adapt),
                    ]
                    for to, of in loads:
                        sp.dma_start(to, of).then_inc(s_in, 16)
                    row = lambda a: a.rearrange("(a d) -> a d", a=1)
                    for k, a in enumerate((b0, gamma, beta, cheb_bias)):
                        sp.dma_start(rows[:, k, :], row(a).to_broadcast([P, D])).then_inc(s_in, 16)
                    for k in range(K):
                        sp.dma_start(b2_rep[:, k, :], row(b2)).then_inc(s_in, 16)
                    sp.wait_ge(v, mark["fill"])
                    per = QC // 25
                    view = rec_dram.rearrange("(p n) f -> p (n f)", p=P)
                    with sp.Fori(0, per) as n:
                        sp.dma_start(view[:, bass.ds(n * (25 * REC), 25 * REC)],
                                     fill[:, :, :].rearrange("p a b -> p (a b)")).then_inc(s_fill, 16)
                    sp.wait_ge(v, mark["src used"])
                    sp.dma_start(wf, edge_weight.rearrange("(p n) -> p n", p=P)).then_inc(s_edge, 16)
                @block.gpsimd
                def _(pool):
                    pool.iota(iota[:, :], [[1, P]], base=0, channel_multiplier=0,
                              allow_small_or_imprecise_dtypes=True).then_inc(s_iota, 1)
                    pool.iota(pcol[:, :], [[0, 1]], base=0, channel_multiplier=1,
                              allow_small_or_imprecise_dtypes=True).then_inc(s_iota, 1)
                    pool.iota(cols[:, :], [[1, 512]], base=0, channel_multiplier=0,
                              allow_small_or_imprecise_dtypes=True).then_inc(s_iota, 1)

                @block.scalar
                def _(act):
                    act.wait_ge(v, mark["remainder"])
                    act.activation(emeta[:, :, CW], wf2, ACT.Sin, bias=half_pi[:, :],
                                   scale=-pi / CUTOFF).then_inc(s_pe, 1)


            with nc.Block() as block:
                @block.vector
                def _(dve):
                    c = chain(dve)
                    dve.wait_ge(s_in, 16 * NIN)
                    c.step(dve.tensor_copy(nodes_w[:, 0, :], types_w[:, :]))
                    mark["types"] = c.n
                    c.step(dve.tensor_scalar(junk_v, emeta[:, :, DWIN], 0.0, None, ALU.is_ge, ALU.add,
                                             accum_out=ge_d[:, 0:1]))
                    keep(c)
                    with dve.Fori(1, W) as w:
                        dve.wait_ge(v, w + (c.n - 1))
                        dve.tensor_scalar(junk_v, emeta[:, :, DWIN], iota[:, bass.ds(w, 1)], None,
                                          ALU.is_ge, ALU.add, accum_out=ge_d[:, bass.ds(w, 1)]).then_inc(v, 1)
                    c.n += W - 1
                    c.done()
                    keep(c)

                @block.scalar
                def _(act):
                    act.activation(wf2, emeta[:, :, SWIN], ACT.Sign, bias=near[:, 0:1], scale=1.0,
                                   accum_out=ge_s[:, 0:1]).then_inc(s_ge, 1)
                    with act.Fori(1, W) as w:
                        act.wait_ge(s_ge, w)
                        act.activation(wf2, emeta[:, :, SWIN], ACT.Sign, bias=near[:, bass.ds(w, 1)],
                                       scale=1.0, accum_out=ge_s[:, bass.ds(w, 1)]).then_inc(s_ge, 1)
                    act.wait_ge(s_ge, W)

                @block.tensor
                def _(pe):
                    pe.wait_ge(v, mark["types"])
                    pe.transpose(ps[0][0:R, 0:D], w_rows[:, 0, 0:R], ident[0:D, 0:D])
                    pe.transpose(ps[1][0:D, 0:D], w_rows[:, 1, :], ident[0:D, 0:D])
                    pe.transpose(ps[2][0:G, 0:P], emb_sb[:, :], ident[:, :])
                    pe.transpose(ps[3][0:G, 0:G], adapt_sb[:, :], ident[0:G, 0:G])
                    for k in range(2):
                        last = pe.transpose(ps[4 + k][0:P, 0:W], nodes_w[0:W, k, :], ident[0:W, 0:W])
                    last.then_inc(s_ready, 1)

            with nc.Block() as block:
                @block.vector
                def _(dve):
                    c = chain(dve)
                    dve.wait_ge(s_ready, 1)
                    c(dve.tensor_copy(w1t[:, :], ps[0][0:R, 0:D]))
                    c(dve.tensor_copy(w2t[:, :], ps[1][0:D, 0:D]))
                    c(dve.tensor_copy(emb_t[:, :], ps[2][0:G, 0:P]))
                    c(dve.tensor_copy(adapt_t[:, :], ps[3][0:G, 0:G]))
                    c(dve.tensor_copy(types_i[:, :], ps[4][:, 0:W]))
                    c(dve.tensor_copy(mult[:, :], ps[5][:, 0:W]))
                    c(dve.tensor_scalar(ge_s[:, :], ge_s[:, :], float(EC), 0.5, ALU.add, ALU.mult))
                    c(dve.tensor_copy(two[:, 0:G], emb_sb[:, :]))
                    mark["transposed"] = c.n
                    dve.wait_ge(s_pe, 2)
                    c.step(dve.tensor_copy(two[:, G:2 * G], ps[6][:, 0:G]))
                    mark["two"] = c.n
                    c(dve.tensor_copy(cnt[:, 0, 0:W], ps[7][:, 0:W]))
                    c.step(dve.tensor_copy(cnt[:, 1, 0:W], ps[7][:, 256:256 + W]))
                    c.step(dve.tensor_tensor(nb[:, :, :], cnt[:, :, 0:W], cnt[:, :, 1:W + 1], ALU.subtract))
                    c(dve.tensor_scalar(cnt_i[:, 0, :], nb[:, 0, :], float(P - 1), None, ALU.add))
                    c.step(dve.tensor_scalar(cnt_i[:, 1, :], nb[:, 1, :], float(SB * P - 1), None, ALU.add))
                    c(dve.tensor_scalar(cnt_i[:, 0, :], cnt_i[:, 0, :], P.bit_length() - 1, None, ALU.logical_shift_right))
                    c.step(dve.tensor_scalar(cnt_i[:, 1, :], cnt_i[:, 1, :], (SB * P).bit_length() - 1, None,
                                             ALU.logical_shift_right))
                    c.step(dve.tensor_copy(nb[:, :, :], cnt_i[:, :, :]))
                    for k in range(2):
                        c(dve.tensor_tensor_scan(inc[:, k, :], ones_f[:, 0:W], nb[:, k, :], 0.0, ALU.mult, ALU.add))
                    c.done()
                    c.step(dve.tensor_tensor(begin[:, :, :], inc[:, :, :], nb[:, :, :], ALU.subtract))
                    c(dve.tensor_scalar(run_d[:, :], begin[:, 0, :], float(P), None, ALU.mult))
                    c(dve.tensor_scalar(run_s[:, :], begin[:, 1, :], float(SB * P), None, ALU.mult))
                    for k in range(2):
                        c.step(dve.tensor_tensor(sel[0:W, :], begin[0:W, k, :], ident[0:W, 0:W], ALU.mult))
                        c.step(dve.tensor_reduce(begin_col[0:W, k:k + 1], sel[0:W, :], AX.X, ALU.add))
                    n = 0
                    for k, (row, count) in enumerate(((win_d, QC), (win_s, SG))):
                        for a in range(0, count, 512):
                            m = min(512, count - a)
                            c.step(dve.tensor_scalar(sel[0:W, 0:1], begin_col[0:W, k:k + 1], float(-a), None, ALU.add))
                            c.step(dve.tensor_scalar(started[0:W, 0:m], cols[0:W, 0:m], sel[0:W, 0:1], None, ALU.is_ge))
                            mark["started", n] = c.n
                            dve.wait_ge(s_uv, 1 + n)
                            c.step(dve.tensor_scalar(row[:, a:a + m], ps[0][0:1, 0:m], -1.0, None, ALU.add))
                            n += 1
                    keep(c)

                @block.sync
                def _(sp):
                    sp.wait_ge(v, mark["two"])
                    sp.dma_start(types_dram, two[0:NT, :]).then_inc(s_out, 16)
                    sp.wait_ge(s_out, 16)
                    sp.wait_ge(s_fill, 16 * (QC // 25))

                @block.tensor
                def _(pe):
                    pe.wait_ge(v, mark["transposed"])
                    pe.matmul(ps[6][:, 0:G], emb_t[:, :], adapt_t[:, :], start=True, stop=True)
                    pe.matmul(ps[7][:, 0:W], ones_f[:, :], ge_d[:, :], start=True, stop=True)
                    pe.matmul(ps[7][:, 256:256 + W], ones_f[:, :], ge_s[:, :], start=True, stop=True).then_inc(s_pe, 1)
                    n = 0
                    for count in (QC, SG):
                        for a in range(0, count, 512):
                            m = min(512, count - a)
                            pe.wait_ge(v, mark["started", n])
                            pe.matmul(ps[0][0:1, 0:m], ones_b[0:W, 0:1], started[0:W, 0:m],
                                      start=True, stop=True).then_inc(s_uv, 1)
                            n += 1

        PS_TOT = W

        def rank_pe(pe, onehot, pos, tot):
            pe.matmul(pos, lt_b[:, :], onehot, start=True, stop=False, skip_group_check=True)
            for j in range(K - 1):
                later = onehot[:, j:j + 1, :].to_broadcast([P, K - 1 - j, W])
                pe.matmul(pos[:, j + 1:K, :], ones_b[:, :], later, start=False, stop=(j == K - 2),
                          skip_group_check=True)
            for j in range(K):
                last = pe.matmul(tot, ones_b[:, :], onehot[:, j, :], start=(j == 0), stop=(j == K - 1),
                                 skip_group_check=True)
            return last

        with ExitStack() as s1:
            recb = scoped(s1, "recb", [P, RING, K, REC], F32)
            row_i = scoped(s1, "row_i", [P, RING, K], I32)
            pos = [s1.enter_context(nc.psum_tensor(f"ps1_{g}", [P, 512], F32)) for g in range(RING)]
            tot = s1.enter_context(nc.psum_tensor("ps1_tot", [P, 512], F32))
            ld, put = sems("s1_attr"), sems("s1_put")
            meta, oh, rk = (sem(f"s1_{n}") for n in ("meta", "onehot", "rank"))
            tot_free = sem("s1_tot_free")
            base_v = vn[0]
            attr = edge_attr.rearrange("(p n) f -> p n f", p=P)

            with nc.Block() as block:
                @block.sync
                def _(sp):
                    def turn(i, first):
                        for g in range(RING):
                            if not first:
                                sp.wait_ge(put[g], i * (16 * K))
                            sp.dma_start(recb[:, g, :, 0:R],
                                         attr[:, bass.ds(i * U + g * K, K), :]).then_inc(ld[g], 16)
                    turns(sp, ET, turn)

                @block.scalar
                def _(act):
                    def turn(i, first):
                        for g in range(RING):
                            if not first:
                                act.wait_ge(put[g], i * (16 * K))
                            act.copy(recb[:, g, :, R:REC],
                                     emeta[:, bass.ds(i * U + g * K, K), :]).then_inc(meta, 1)
                    turns(act, ET, turn)

                def pos_of(g):
                    return pos[g][:, 0:K * W].rearrange("p (k w) -> p k w", k=K)

                @block.vector
                def _(dve):
                    c = chain(dve)
                    base = base_v

                    def finish(i, g):
                        dve.wait_ge(rk, i * RING + (g + 1))
                        rank_dve_steps(i, g)

                    def rank_dve_steps(i, g):
                        at = lambda k: i * (3 * RING) + (base + 3 * g + k)
                        dve.wait_ge(v, at(0))
                        dve.tensor_tensor(rank[:, :, :], pos_of(g),
                                          run_d[:, :].unsqueeze(1).to_broadcast([P, K, W]), ALU.add).then_inc(v, 1)
                        dve.wait_ge(v, at(1))
                        dve.tensor_tensor(run_d[:, :], run_d[:, :], tot[:, 0:W], ALU.add).then_inc(tot_free, 1)
                        dve.tensor_tensor(rank[:, :, :], rank[:, :, :], onehot_w[:, g, :, :], ALU.mult).then_inc(v, 1)
                        dve.wait_ge(v, at(2))
                        with nc.allow_low_precision(reason="row numbers: whole, below 2^24"):
                            dve.tensor_reduce(row_i[:, g, :], rank[:, :, :], AX.X, ALU.add).then_inc(v, 1)

                    def turn(i, first):
                        for g in range(RING):
                            dve.wait_ge(meta, i * RING + (g + 1))
                            for k in range(K):
                                last = dve.tensor_scalar(onehot_w[:, g, k, :], iota_b[:, 0:W],
                                                         recb[:, g, k, R + DWIN:R + DWIN + 1], None, ALU.is_equal)
                            last.then_inc(oh, 1)
                            if g:
                                finish(i, g - 1)
                            elif not first:
                                finish(i - 1, RING - 1)
                    turns(dve, ET, turn)
                    finish(ET - 1, RING - 1)
                    c.n = base + 3 * RING * ET
                    keep(c)

                @block.tensor
                def _(pe):
                    def turn(i, first):
                        for g in range(RING):
                            pe.wait_ge(oh, i * RING + (g + 1))
                            if not first or g:
                                pe.wait_ge(tot_free, i * RING + g)
                            rank_pe(pe, onehot_w[:, g, :, :], pos_of(g), tot[:, 0:W]).then_inc(rk, 1)
                    turns(pe, ET, turn)

                @block.gpsimd
                def _(pool):
                    def turn(i, first):
                        for g in range(RING):
                            lone_wait(pool, v, i * (3 * RING) + (base_v + 3 * g + 3))
                            lone_wait(pool, ld[g], i * 16 + 16)
                            for k in range(K):
                                pool.indirect_dma_start(
                                    rec_dram, bass.IndirectOffsetOnAxis(ap=row_i[:, g, k:k + 1], axis=0),
                                    recb[:, g, k, :], None).then_inc(put[g], 16)
                    turns(pool, ET, turn)
                    for g in range(RING):
                        pool.wait_ge(put[g], ET * 16 * K)
        edges.close()

        X = sb("X", [P, W, D])
        s_node = sem("node_act")
        s_dma = sem("node_dma")
        n_node, n_dma = [0], [0]

        def over_features(a):
            return a.unsqueeze(2).to_broadcast([P, W, D])

        class Node:

            def __init__(self, dve):
                self.dve, self.c, self.acts, self.stores = dve, chain(dve), [], []

            def sqrt(self, a):
                self.acts.append((self.c.n, a, n_node[0]))
                n_node[0] += 1
                self.dve.wait_ge(s_node, n_node[0])

            def store(self, to, of):
                self.stores.append((self.c.n, to, of))
                n_dma[0] += 16

            def layernorm(self, to, of, square, relu):
                c, dve = self.c, self.dve
                c.step(dve.tensor_reduce(mean[:, :], of, AX.X, ALU.add))
                c.step(dve.tensor_scalar(mean[:, :], mean[:, :], 1.0 / D, None, ALU.mult))
                c.step(dve.tensor_tensor(to, of, over_features(mean[:, :]), ALU.subtract))
                c.step(dve.tensor_tensor(square, to, to, ALU.mult))
                c.step(dve.tensor_reduce(var[:, :], square, AX.X, ALU.add))
                c.step(dve.tensor_scalar(var[:, :], var[:, :], 1.0 / D, LN_EPS, ALU.mult, ALU.add))
                self.sqrt(var[:, :])
                c.step(dve.reciprocal(var[:, :], var[:, :]))
                c.step(dve.tensor_tensor(to, to, over_features(var[:, :]), ALU.mult))
                if relu:
                    c.step(dve.tensor_scalar(to, to, 0.0, None, ALU.max))

        def node_block(steps, pool_steps=None, before=()):
            with nc.Block() as block:
                node = []

                @block.vector
                def _(dve):
                    node.append(Node(dve))
                    if before:
                        n_dma[0] += 16 * len(before)
                        dve.wait_ge(s_dma, n_dma[0])
                    steps(node[0], node[0].c, dve)
                    keep(node[0].c)

                @block.scalar
                def _(act):
                    for at, a, _ in node[0].acts:
                        act.wait_ge(v, at)
                        act.activation(a, a, ACT.Sqrt).then_inc(s_node, 1)

                @block.sync
                def _(sp):
                    for to, of in before:
                        sp.dma_start(to, of).then_inc(s_dma, 16)
                    for at, to, of in node[0].stores:
                        sp.wait_ge(v, at)
                        sp.dma_start(to, of).then_inc(s_dma, 16)
                    if before or node[0].stores:
                        sp.wait_ge(s_dma, n_dma[0])

                if pool_steps is not None:
                    @block.gpsimd
                    def _(pool):
                        pool_steps(pool)

        PW = 7
        PT = W // (2 * PW)
        assert W == 2 * PW * PT
        pj = {n: [sem(f"pj_{n}{s}") for s in range(2)] for n in ("stage", "trans", "lhs", "prod", "out")}
        n_pj = [0]

        def project(rows_of, matrix, put):
            base = PT * n_pj[0]
            n_pj[0] += 1
            with ExitStack() as s:
                stage = scoped(s, f"stage{n_pj[0]}", [P, 2, PW, D], F32)
                lhs = scoped(s, f"lhs{n_pj[0]}", [D, 2, PW * P], F32)
                pst = s.enter_context(nc.psum_tensor(f"pst{n_pj[0]}", [P, 2, 1024], F32))
                pso = s.enter_context(nc.psum_tensor(f"pso{n_pj[0]}", [P, 2, 512], F32))
                with nc.Block() as block:
                    @block.scalar
                    def _(act):
                        def turn(i, first):
                            for q in range(2):
                                if not first:
                                    act.wait_ge(pj["trans"][q], i + base)
                                act.copy(stage[:, q, :, :], rows_of[:, bass.ds((i * 2 + q) * PW, PW), :]
                                         ).then_inc(pj["stage"][q], 1)
                                act.wait_ge(pj["trans"][q], i + (base + 1))
                                if not first:
                                    act.wait_ge(pj["prod"][q], i + base)
                                act.copy(lhs[:, q, :], pst[0:D, q, 0:PW * P]).then_inc(pj["lhs"][q], 1)
                        turns(act, PT, turn)

                    @block.tensor
                    def _(pe):
                        def turn(i, first):
                            for q in range(2):
                                pe.wait_ge(pj["stage"][q], i + (base + 1))
                                if not first:
                                    lone_wait(pe, pj["lhs"][q], i + base)
                                for n in range(PW):
                                    last = pe.transpose(pst[0:D, q, n * P:(n + 1) * P], stage[:, q, n, :],
                                                        ident[:, :])
                                last.then_inc(pj["trans"][q], 1)
                                pe.wait_ge(pj["lhs"][q], i + (base + 1))
                                if not first:
                                    pe.wait_ge(pj["out"][q], i + base)
                                for n in range(PW):
                                    last = pe.matmul(pso[:, q, n * D:(n + 1) * D],
                                                     lhs[:, q, n * P:(n + 1) * P], matrix,
                                                     start=True, stop=True)
                                last.then_inc(pj["prod"][q], 1)
                        turns(pe, PT, turn)

                    @block.vector
                    def _(dve):
                        def turn(i, first):
                            for q in range(2):
                                dve.wait_ge(pj["prod"][q], i + (base + 1))
                                put(dve, pso[:, q, 0:PW * D].rearrange("p (w f) -> p w f", w=PW),
                                    (i * 2 + q) * PW).then_inc(pj["out"][q], 1)
                        turns(dve, PT, turn)

        full = (W - 1) * P
        meta = sb("meta", [P, QC, 4])
        hv_scope = ExitStack()
        hv = scoped(hv_scope, "hv", [P, W, HV], F32)
        with ExitStack() as s2:
            tab0 = scoped(s2, "tab0", [P, W, T0], F32)
            h = scoped(s2, "h0", [P, W, D], F32)
            spare = meta[:, :, :].rearrange("p n f -> p (n f)")
            square = spare[:, 0:W * D].rearrange("p (w f) -> p w f", w=W)
            uv = spare[:, W * D:W * (D + 2 * G)].rearrange("p (w f) -> p w f", w=W)
            s_x0, s_uvg = sem("x_zeroed"), sem("types_gathered")

            with nc.Block() as block:
                @block.vector
                def _(dve):
                    dve.memset(X[:, :, :], 0.0).then_inc(s_x0, 1)

            def types_of_nodes(pool):
                for w in range(W):
                    pool.indirect_dma_start(
                        uv[:, w, :], None, types_dram,
                        bass.IndirectOffsetOnAxis(ap=types_i[:, w:w + 1], axis=0)).then_inc(s_uvg, 16)
                pool.wait_ge(s_uvg, 16 * W)

            def steps(node, c, dve):
                node.layernorm(h[:, :, :], X[:, :, :], square[:, :, :], True)
                dve.wait_ge(s_uvg, 16 * W)
                c(dve.tensor_copy(tab0[:, :, D:T0], uv[:, :, 0:G]))
                c(dve.tensor_copy(hv[:, :, D:D + G], uv[:, :, G:2 * G]))
                c(dve.tensor_copy(hv[:, :, D + G], mult[:, :]))
                c.done()

            node_block(steps, types_of_nodes,
                       before=[(X[:, 0:W - 1, :], x[0:full].rearrange("(w p) f -> p w f", p=P)),
                               (X[0:TAIL, W - 1, :], x[full:N])])
            project(h, w0_sb[:, :], lambda dve, of, w: dve.tensor_copy(tab0[:, bass.ds(w, PW), 0:D], of))
            node_block(lambda node, c, dve: node.store(
                tab0_dram.rearrange("(p w) f -> p (w f)", p=P), tab0[:, :, :].rearrange("p w f -> p (w f)")))

        rows_scope = ExitStack()
        src_row = scoped(rows_scope, "src_row", [P, QC], I32)
        pg_dma = sems("prop_gather")
        pg_st, pg_oh, pg_mm = (sem(f"prop_{n}") for n in ("staged", "onehot", "sum"))
        n_prop = [0]

        def windows(engine_type, row, at, count):
            return nc.values_load_multi_w_load_instructions(
                row[0:1, bass.ds(at, count)], engines=(engine_type,), min_val=0, max_val=W - 1,
                skip_runtime_bounds_check_because="windows are counted below W")[1]

        def propagate(table, width, weight, acc, first_layer):
            n = n_prop[0]
            n_prop[0] += 1
            base = n * QT
            per = K + (4 if first_layer else 0)
            with ExitStack() as s:
                gath = scoped(s, f"gath{n}", [P, RING, K, width], F32)
                onehot = scoped(s, f"onehot{n}", [P, RING, K, P], F32)
                idx_s = scoped(s, f"idx_s{n}", [P, RING, K], I32)
                fields = scoped(s, f"fields{n}", [P, RING, K, NF if first_layer else 4], F32)
                sums = s.enter_context(nc.psum_tensor(f"sums{n}", [P, RING, 512], F32))
                acc_flat = acc[:, :, :].rearrange("p w f -> p (w f)")
                if first_layer:
                    pad = scoped(s, "pad", [P, K], F32)
                    rank_sum = scoped(s, "rank_sum", [P, K], F32)
                    pos = s.enter_context(nc.psum_tensor("pos", [P, 2, 512], F32))
                    tot_bank = s.enter_context(nc.psum_tensor("tot_src", [P, 512], F32))
                    ld, us = sems("fields_load"), sems("types_save")
                    woh, rk = sem("windows_onehot"), sem("windows_rank")
                    u_view = u_dram.rearrange("p (n f) -> p n f", f=G)
                    rec_view = rec_dram.rearrange("(n p) f -> p n f", p=P)
                    tot = tot_bank[:, 0:W]

                def sum_of(g):
                    return sums[:, g, 0:K * D]

                def pos_of(g):
                    return pos[:, g % 2, 0:K * W].rearrange("p (k w) -> p k w", k=K)

                with nc.Block() as block:
                    @block.vector
                    def _(dve):
                        c = chain(dve)
                        c.step(dve.memset(acc_flat, 0.0))
                        keep(c)
                    mark["prop"] = vn[0]
                b_v = vn[0]

                def v_at(i, g, k):
                    return i * (per * RING) + (b_v + per * g + k)

                with nc.Block() as block:
                    if first_layer:
                        @block.sync
                        def _(sp):
                            def turn(i, first):
                                for g in range(RING):
                                    if not first:
                                        lone_wait(sp, v, v_at(i - 1, g, per))
                                        lone_wait(sp, pg_st, i * RING + (base * RING + g + 1 - RING))
                                    sp.dma_start(fields[:, g, :, :],
                                                 rec_view[:, bass.ds(i * U + g * K, K), R:REC]).then_inc(ld[g], 16)
                                for g in range(RING):
                                    lone_wait(sp, pg_dma[g], (i + (base + 1)) * (16 * K))
                                    sp.dma_start(u_view[:, bass.ds(i * U + g * K, K), :],
                                                 gath[:, g, :, D:T0]).then_inc(us[g], 16)
                            turns(sp, QT, turn)
                            for g in range(RING):
                                sp.wait_ge(us[g], 16 * QT)

                    @block.scalar
                    def _(act):
                        def turn(i, first):
                            for g in range(RING):
                                at = bass.ds(i * U + g * K, K)
                                if not first:
                                    act.wait_ge(pg_dma[g], (i + base) * (16 * K))
                                if first_layer:
                                    act.wait_ge(ld[g], i * 16 + 16)
                                    act.copy(meta[:, at, :], fields[:, g, :, 0:4])
                                    act.copy(idx_s[:, g, :], fields[:, g, :, IDX]).then_inc(pg_st, 1)
                                else:
                                    if not first:
                                        act.wait_ge(pg_oh, i * RING + (base * RING + g + 1 - RING))
                                    act.copy(fields[:, g, :, :], meta[:, at, :])
                                    act.copy(idx_s[:, g, :], meta[:, at, IDX]).then_inc(pg_st, 1)
                        turns(act, QT, turn)

                    @block.gpsimd
                    def _(pool):
                        def turn(i, first):
                            for g in range(RING):
                                lone_wait(pool, pg_st, i * RING + (base * RING + g + 1))
                                if not first:
                                    lone_wait(pool, pg_mm, i * RING + (base * RING + g + 1 - RING))
                                    if first_layer:
                                        lone_wait(pool, us[g], i * 16)
                                for k in range(K):
                                    pool.indirect_dma_start(
                                        gath[:, g, k, :], None, table,
                                        bass.IndirectOffsetOnAxis(ap=idx_s[:, g, k:k + 1], axis=0)
                                    ).then_inc(pg_dma[g], 16)
                        turns(pool, QT, turn)

                    @block.vector
                    def _(dve):
                        def finish(i, g):
                            ws = windows(DVE_ENGINE, win_d, i * U + g * K, K)
                            dve.wait_ge(pg_mm, i * RING + (base * RING + g + 1))
                            for k in range(K):
                                to = acc_flat[:, bass.ds(ws[k] * D, D)]
                                dve.wait_ge(v, v_at(i, g, k))
                                dve.tensor_tensor(to, to, sum_of(g)[:, k * D:(k + 1) * D], ALU.add).then_inc(v, 1)
                            if not first_layer:
                                return
                            dve.wait_ge(rk, i * RING + (g + 1))
                            dve.wait_ge(v, v_at(i, g, K))
                            dve.tensor_tensor(rank[:, :, :], pos_of(g),
                                              run_s[:, :].unsqueeze(1).to_broadcast([P, K, W]), ALU.add)
                            dve.tensor_scalar(pad[:, :], fields[:, g, :, SWIN], 0.0, OUT_OF_BOUNDS,
                                              ALU.is_lt, ALU.mult).then_inc(v, 1)
                            dve.wait_ge(v, v_at(i, g, K + 1))
                            dve.tensor_tensor(run_s[:, :], run_s[:, :], tot, ALU.add)
                            dve.tensor_tensor(rank[:, :, :], rank[:, :, :], onehot_w[:, g, :, :],
                                              ALU.mult).then_inc(v, 1)
                            dve.wait_ge(v, v_at(i, g, K + 2))
                            dve.tensor_reduce(rank_sum[:, :], rank[:, :, :], AX.X, ALU.add).then_inc(v, 1)
                            dve.wait_ge(v, v_at(i, g, K + 3))
                            dve.tensor_tensor(src_row[:, bass.ds(i * U + g * K, K)], rank_sum[:, :], pad[:, :],
                                              ALU.add).then_inc(v, 1)

                        def turn(i, first):
                            for g in range(RING):
                                if first_layer:
                                    dve.wait_ge(ld[g], i * 16 + 16)
                                else:
                                    dve.wait_ge(pg_st, i * RING + (base * RING + g + 1))
                                if not first:
                                    dve.wait_ge(pg_mm, i * RING + (base * RING + g + 1 - RING))
                                f = fields[:, g, :, :]
                                for k in range(K):
                                    last = dve.tensor_scalar(onehot[:, g, k, :], iota[:, :], f[:, k, DREL:DREL + 1],
                                                             f[:, k, weight:weight + 1], ALU.is_equal, ALU.mult)
                                last.then_inc(pg_oh, 1)
                                if first_layer:
                                    for k in range(K):
                                        last = dve.tensor_scalar(onehot_w[:, g, k, :], iota_b[:, 0:W],
                                                                 f[:, k, SWIN:SWIN + 1], None, ALU.is_equal)
                                    last.then_inc(woh, 1)
                                if g:
                                    finish(i, g - 1)
                                elif not first:
                                    finish(i - 1, RING - 1)
                        turns(dve, QT, turn)
                        finish(QT - 1, RING - 1)
                        vn[0] = b_v + per * RING * QT

                    @block.tensor
                    def _(pe):
                        def turn(i, first):
                            for g in range(RING):
                                if first_layer:
                                    pe.wait_ge(woh, i * RING + (g + 1))
                                    if g:
                                        pe.wait_ge(v, v_at(i, g - 1, per))
                                    elif not first:
                                        pe.wait_ge(v, v_at(i - 1, RING - 1, per))
                                    rank_pe(pe, onehot_w[:, g, :, :], pos_of(g), tot).then_inc(rk, 1)
                                pe.wait_ge(pg_oh, i * RING + (base * RING + g + 1))
                                pe.wait_ge(pg_dma[g], (i + (base + 1)) * (16 * K))
                                if not first:
                                    pe.wait_ge(v, v_at(i - 1, g, per))
                                for k in range(K):
                                    last = pe.matmul(sum_of(g)[:, k * D:(k + 1) * D], onehot[:, g, k, :],
                                                     gath[:, g, k, 0:D], start=True, stop=True)
                                last.then_inc(pg_mm, 1)
                        turns(pe, QT, turn)

        with ExitStack() as s3:
            acc = scoped(s3, "acc0", [P, W, D], F32)
            square = acc
            propagate(tab0_dram, T0, EW, acc, True)

            def steps(node, c, dve):
                c.step(dve.tensor_tensor(acc[:, :, :], acc[:, :, :],
                                         rows[:, B0, :].unsqueeze(1).to_broadcast([P, W, D]), ALU.add))
                c.step(dve.scalar_tensor_tensor(out=X[:, :, :], in0=acc[:, :, :], scalar=0.0, in1=X[:, :, :],
                                                op0=ALU.max, op1=ALU.add))
                node.layernorm(hv[:, :, 0:D], X[:, :, :], square[:, :, :], True)

            node_block(steps)

        with ExitStack() as s4:
            recl = scoped(s4, "recl", [P, RING, K, REC], F32)
            ul = scoped(s4, "ul", [P, RING, K, G], F32)
            row_s = scoped(s4, "row_s", [P, RING, K], I32)
            oh_b = scoped(s4, "oh_b", [P, RING, K, P], BF16)
            oht = scoped(s4, "oht", [P, RING, K, P], F32)
            ident_b = scoped(s4, "ident_b", [P, P], BF16)
            attr_t = scoped(s4, "attr_t", [R, RING, K * P], F32)
            act1 = scoped(s4, "act1", [D, RING, K * P], F32)
            msgs = scoped(s4, "msgs", [P, RING, K, MSG], F32)
            uxv = scoped(s4, "uxv", [P, K, G], F32)
            logit = scoped(s4, "logit", [P, K], F32)
            scale = scoped(s4, "scale", [P, K], F32)
            gate_s = scoped(s4, "gate_s", [P, K, D], F32)
            fill = scoped(s4, "fill_src", [P, 8, MSG], F32)
            ps_oht = s4.enter_context(nc.psum_tensor("ps_oht", [P, K * P], BF16))
            ps_at = s4.enter_context(nc.psum_tensor("ps_at", [P, 1024], F32))
            ps_h1 = s4.enter_context(nc.psum_tensor("ps_h1", [P, 1024], F32))
            ps_gate = s4.enter_context(nc.psum_tensor("ps_gate", [P, 512], F32))
            ps_hv = s4.enter_context(nc.psum_tensor("ps_hv", [P, 512], F32))
            ld, ldu, put = sems("l1_load"), sems("l1_types"), sems("l1_put")
            ohb, tr, cp, st, h1s, si, hvs, gt = (
                sem(f"l1_{n}") for n in ("onehot", "trans", "copied", "staged", "hidden", "silu", "dstrow", "gate"))
            s_pad = sem("l1_padding")
            hv_flat = hv[:, :, :].rearrange("p w f -> p (w f)")
            rec_view = rec_dram.rearrange("(n p) f -> p n f", p=P)
            u_view = u_dram.rearrange("p (n f) -> p n f", f=G)
            pads = SROWS // P // 8

            with nc.Block() as block:
                @block.vector
                def _(dve):
                    c = chain(dve)
                    c(dve.memset(fill[:, :, :], 0.0))
                    c(dve.memset(msgs[:, :, :, :].rearrange("p a b f -> p (a b f)"), 0.0))
                    c(dve.tensor_copy(ident_b[:, :], ident[:, :]))
                    c.done()
                    c.step(dve.memset(fill[:, :, MREL:MREL + 1], -1.0))
                    mark["l1"] = c.n
                    keep(c)

                @block.sync
                def _(sp):
                    sp.wait_ge(v, mark["l1"])
                    view = msg_dram.rearrange("(p n) f -> p (n f)", p=P)
                    with sp.Fori(0, pads) as n:
                        sp.dma_start(view[:, bass.ds(n * (8 * MSG), 8 * MSG)],
                                     fill[:, :, :].rearrange("p a b -> p (a b)")).then_inc(s_pad, 16)
                    sp.wait_ge(s_pad, 16 * pads)

            b_v = vn[0]
            per = 6

            def v_at(i, g, k):
                return i * (per * RING) + (b_v + per * g + k)

            with nc.Block() as block:
                @block.sync
                def _(sp):
                    def turn(i, first):
                        for g in range(RING):
                            if not first:
                                lone_wait(sp, v, v_at(i - 1, g, per))
                                lone_wait(sp, st, i * RING + (g + 1 - RING))
                                lone_wait(sp, tr, i * RING + (g + 1 - RING))
                            at = bass.ds(i * U + g * K, K)
                            sp.dma_start(recl[:, g, :, :], rec_view[:, at, :]).then_inc(ld[g], 16)
                            sp.dma_start(ul[:, g, :, :], u_view[:, at, :]).then_inc(ldu[g], 16)
                    turns(sp, QT, turn)

                @block.scalar
                def _(act):
                    def hidden(i, g):
                        act.wait_ge(h1s, i * RING + (g + 1))
                        act.activation(act1[:, g, :], ps_h1[0:D, 0:K * P], ACT.Silu, bias=b1_col[:, :],
                                       scale=1.0).then_inc(si, 1)

                    def turn(i, first):
                        for g in range(RING):
                            if not first:
                                act.wait_ge(put[g], i * (16 * K))
                                act.wait_ge(gt, i * RING + (g + 1 - RING))
                            act.wait_ge(ld[g], i * 16 + 16)
                            act.copy(row_s[:, g, :], src_row[:, bass.ds(i * U + g * K, K)])
                            act.copy(msgs[:, g, :, DEG], recl[:, g, :, R + EW3])
                            act.copy(msgs[:, g, :, MREL], recl[:, g, :, R + SREL]).then_inc(st, 1)
                            act.wait_ge(tr, i * RING + (g + 1))
                            act.copy(attr_t[:, g, :], ps_at[0:R, 0:K * P])
                            act.copy(oht[:, g, :, :].rearrange("p k e -> p (k e)"),
                                     ps_oht[:, :]).then_inc(cp, 1)
                            if g:
                                hidden(i, g - 1)
                            elif not first:
                                hidden(i - 1, RING - 1)
                    turns(act, QT, turn)
                    hidden(QT - 1, RING - 1)

                @block.tensor
                def _(pe):
                    def transposes(i, first, g):
                        pe.wait_ge(ohb, i * RING + (g + 1))
                        if g:
                            lone_wait(pe, cp, i * RING + g)
                        elif not first:
                            lone_wait(pe, cp, i * RING)
                        for k in range(K):
                            pe.transpose(ps_oht[:, k * P:(k + 1) * P], oh_b[:, g, k, :], ident_b[:, :])
                        for k in range(K):
                            last = pe.transpose(ps_at[0:R, k * P:(k + 1) * P], recl[:, g, k, 0:R], ident[:, :])
                        last.then_inc(tr, 1)

                    def products(i, first, g):
                        ws = windows(PE_ENGINE, win_d, i * U + g * K, K)
                        pe.wait_ge(cp, i * RING + (g + 1))
                        if g:
                            pe.wait_ge(si, i * RING + g)
                        elif not first:
                            pe.wait_ge(si, i * RING)
                        pe.nop(nofuse=True)
                        for a, b in ((0, 512), (512, K * P)):
                            last = pe.matmul(ps_h1[0:D, a:b], w1t[:, :], attr_t[:, g, a:b], start=True, stop=True)
                        last.then_inc(h1s, 1)
                        if g:
                            lone_wait(pe, v, v_at(i, g - 1, per))
                        elif not first:
                            lone_wait(pe, v, v_at(i - 1, RING - 1, per))
                        for k in range(K):
                            last = pe.matmul(ps_hv[:, k * HV:(k + 1) * HV], oht[:, g, k, :],
                                             hv_flat[:, bass.ds(ws[k] * HV, HV)], start=True, stop=True)
                        last.then_inc(hvs, 1)
                        pe.matmul(ps_gate[:, 0:K * D], ones_f[0:1, :], b2_rep[:, :, :].rearrange("a k d -> a (k d)"),
                                  start=True, stop=False, skip_group_check=True)
                        lone_wait(pe, si, i * RING + (g + 1))
                        for k in range(K):
                            last = pe.matmul(ps_gate[:, k * D:(k + 1) * D], act1[:, g, k * P:(k + 1) * P],
                                             w2t[:, :], start=False, stop=(k == K - 1), skip_group_check=True)
                        last.then_inc(gt, 1)

                    def turn(i, first):
                        for g in range(RING):
                            transposes(i, first, g)
                            if g:
                                products(i, first, g - 1)
                            elif not first:
                                products(i - 1, False, RING - 1)
                    turns(pe, QT, turn)
                    products(QT - 1, False, RING - 1)

                @block.vector
                def _(dve):
                    def bc(a, n):
                        return a.unsqueeze(2).to_broadcast([P, K, n])

                    def finish(i, g):
                        hvg = ps_hv[:, 0:K * HV].rearrange("p (k f) -> p k f", k=K)
                        dve.wait_ge(hvs, i * RING + (g + 1))
                        dve.wait_ge(ldu[g], i * 16 + 16)
                        dve.wait_ge(v, v_at(i, g, 0))
                        dve.tensor_tensor(uxv[:, :, :], hvg[:, :, D:D + G], ul[:, g, :, :], ALU.mult)
                        dve.tensor_tensor(scale[:, :], hvg[:, :, D + G], recl[:, g, :, R + CW],
                                          ALU.mult).then_inc(v, 1)
                        dve.wait_ge(v, v_at(i, g, 1))
                        dve.tensor_reduce(logit[:, :], uxv[:, :, :], AX.X, ALU.add).then_inc(v, 1)
                        dve.wait_ge(gt, i * RING + (g + 1))
                        dve.wait_ge(v, v_at(i, g, 2))
                        dve.tensor_tensor(gate_s[:, :, :], ps_gate[:, 0:K * D].rearrange("p (k f) -> p k f", k=K),
                                          bc(logit[:, :], D), ALU.add).then_inc(v, 1)
                        dve.wait_ge(v, v_at(i, g, 3))
                        dve.tensor_tensor(gate_s[:, :, :], gate_s[:, :, :], hvg[:, :, 0:D], ALU.mult).then_inc(v, 1)
                        dve.wait_ge(v, v_at(i, g, 4))
                        dve.tensor_tensor(msgs[:, g, :, 0:D], gate_s[:, :, :], bc(scale[:, :], D),
                                          ALU.mult).then_inc(v, 1)
                        dve.tensor_copy(msgs[:, g, :, TOT], hvg[:, :, D + G]).then_inc(v, 1)

                    def turn(i, first):
                        for g in range(RING):
                            dve.wait_ge(ld[g], i * 16 + 16)
                            if not first:
                                dve.wait_ge(tr, i * RING + (g + 1 - RING))
                                dve.wait_ge(put[g], i * (16 * K))
                            for k in range(K):
                                last = dve.tensor_scalar(oh_b[:, g, k, :], iota_b[:, :],
                                                         recl[:, g, k, R + DREL:R + DREL + 1], None, ALU.is_equal)
                            last.then_inc(ohb, 1)
                            if g:
                                finish(i, g - 1)
                            elif not first:
                                finish(i - 1, RING - 1)
                    turns(dve, QT, turn)
                    finish(QT - 1, RING - 1)
                    vn[0] = b_v + per * RING * QT

                @block.gpsimd
                def _(pool):
                    last_row = pool.to_reg(SROWS - 1)

                    def turn(i, first):
                        for g in range(RING):
                            lone_wait(pool, st, i * RING + (g + 1))
                            lone_wait(pool, v, v_at(i, g, per))
                            for k in range(K):
                                pool.indirect_dma_start(
                                    msg_dram, bass.IndirectOffsetOnAxis(ap=row_s[:, g, k:k + 1], axis=0),
                                    msgs[:, g, k, :], None, bounds_check=last_row,
                                    oob_is_err=False).then_inc(put[g], 16)
                    turns(pool, QT, turn)
                    for g in range(RING):
                        pool.wait_ge(put[g], QT * 16 * K)
        rows_scope.close()

        with ExitStack() as s5:
            acc = scoped(s5, "acc1", [P, W, AC], F32)
            with ExitStack() as s6:
                ml = scoped(s6, "ml", [P, RING, SB, MSG], F32)
                onehot = scoped(s6, "onehot_src", [P, RING, SB, P], F32)
                sums = s6.enter_context(nc.psum_tensor("sums_src", [P, RING, 512], F32))
                ld, ohs, mm = sems("src_load"), sem("src_onehot"), sem("src_sum")
                acc_flat = acc[:, :, :].rearrange("p w f -> p (w f)")
                msg_view = msg_dram.rearrange("(n p k) f -> p n (k f)", p=P, k=SB)
                with nc.Block() as block:
                    @block.vector
                    def _(dve):
                        c = chain(dve)
                        c.step(dve.memset(acc_flat, 0.0))
                        keep(c)
                b_v6 = vn[0]

                def v_at6(i, g, k):
                    return i * RING + (b_v6 + g + k)

                with nc.Block() as block:
                    @block.sync
                    def _(sp):
                        def turn(i, first):
                            for g in range(RING):
                                if not first:
                                    lone_wait(sp, mm, i * RING + (g + 1 - RING))
                                sp.dma_start(ml[:, g, :, :].rearrange("p k f -> p (k f)"),
                                             msg_view[:, bass.ds(i * RING + g, 1), :].rearrange("p a f -> p (a f)")
                                             ).then_inc(ld[g], 16)
                        turns(sp, ST, turn)

                    @block.vector
                    def _(dve):
                        def finish(i, g, w):
                            dve.wait_ge(mm, i * RING + (g + 1))
                            dve.wait_ge(v, v_at6(i, g, 0))
                            to = acc_flat[:, bass.ds(w * AC, AC)]
                            dve.tensor_tensor(to, to, sums[:, g, 0:AC], ALU.add).then_inc(v, 1)

                        def turn(i, first):
                            for g in range(RING):
                                dve.wait_ge(ld[g], i * 16 + 16)
                                if not first:
                                    dve.wait_ge(mm, i * RING + (g + 1 - RING))
                                for k in range(SB):
                                    last = dve.tensor_scalar(onehot[:, g, k, :], iota[:, :],
                                                             ml[:, g, k, MREL:MREL + 1], None, ALU.is_equal)
                                last.then_inc(ohs, 1)
                                if g:
                                    finish(i, g - 1, ws[g - 1])
                                elif not first:
                                    finish(i - 1, RING - 1, windows(DVE_ENGINE, win_s, (i - 1) * RING + RING - 1, 1)[0])
                                if g == 0:
                                    ws = windows(DVE_ENGINE, win_s, i * RING, RING)
                        turns(dve, ST, turn)
                        finish(ST - 1, RING - 1, windows(DVE_ENGINE, win_s, SG - 1, 1)[0])
                        vn[0] = b_v6 + SG

                    @block.tensor
                    def _(pe):
                        def turn(i, first):
                            for g in range(RING):
                                pe.wait_ge(ohs, i * RING + (g + 1))
                                if not first:
                                    pe.wait_ge(v, v_at6(i - 1, g, 1))
                                for k in range(SB):
                                    last = pe.matmul(sums[:, g, 0:AC], onehot[:, g, k, :], ml[:, g, k, 0:AC],
                                                     start=(k == 0), stop=(k == SB - 1))
                                last.then_inc(mm, 1)
                        turns(pe, ST, turn)

            square = scoped(s5, "square1", [P, W, D], F32)
            t = scoped(s5, "t1", [P, W, D], F32)

            def row_of(k):
                return rows[:, k, :].unsqueeze(1).to_broadcast([P, W, D])

            def steps(node, c, dve):
                c.step(dve.tensor_scalar(var[:, :], acc[:, :, TOT], 1e-8, None, ALU.max))
                c.step(dve.reciprocal(var[:, :], var[:, :]))
                c.step(dve.tensor_tensor(t[:, :, :], acc[:, :, 0:D], over_features(var[:, :]), ALU.mult))
                c.step(dve.tensor_tensor(t[:, :, :], t[:, :, :], hv[:, :, 0:D], ALU.add))
                node.layernorm(t[:, :, :], t[:, :, :], square[:, :, :], False)
                c.step(dve.tensor_tensor(t[:, :, :], t[:, :, :], row_of(GAMMA), ALU.mult))
                c.step(dve.tensor_tensor(t[:, :, :], t[:, :, :], row_of(BETA), ALU.add))
                c.step(dve.tensor_tensor(X[:, :, :], X[:, :, :], t[:, :, :], ALU.add))
                c.step(dve.tensor_scalar(dis[:, :], acc[:, :, DEG], 1.0, None, ALU.max))
                node.sqrt(dis[:, :])
                c.step(dve.reciprocal(dis[:, :], dis[:, :]))
                c.step(dve.scalar_tensor_tensor(out=dis[:, :], in0=acc[:, :, DEG], scalar=0.0, in1=dis[:, :],
                                                op0=ALU.is_gt, op1=ALU.mult))

            node_block(steps)
        hv_scope.close()

        tab_view = tab_dram.rearrange("(p w) f -> p (w f)", p=P)

        def flat(a):
            return a[:, :, :].rearrange("p w f -> p (w f)")

        acc = sb("acc", [P, W, D])
        ta = sb("ta", [P, W, D])
        tb = sb("tb", [P, W, D])
        third = 1.0 / 3.0

        def steps(node, c, dve):
            node.layernorm(ta[:, :, :], X[:, :, :], tb[:, :, :], True)
            node.store(tab_view, flat(ta))
            c.step(dve.scalar_tensor_tensor(out=X[:, :, :], in0=ta[:, :, :], scalar=third, in1=X[:, :, :],
                                            op0=ALU.mult, op1=ALU.add))
        node_block(steps)
        for layer in range(2):
            propagate(tab_dram, D, EW, acc, False)

            def steps(node, c, dve):
                if layer == 0:
                    node.store(tab_view, flat(acc))
                c.step(dve.scalar_tensor_tensor(out=X[:, :, :], in0=acc[:, :, :], scalar=third, in1=X[:, :, :],
                                                op0=ALU.mult, op1=ALU.add))
            node_block(steps)

        def add_to_x(dve, of, w):
            at = X[:, bass.ds(w, PW), :]
            return dve.tensor_tensor(at, at, of, ALU.add)

        def steps(node, c, dve):
            node.layernorm(ta[:, :, :], X[:, :, :], tb[:, :, :], True)
            c.step(dve.tensor_tensor(tb[:, :, :], ta[:, :, :], over_features(dis[:, :]), ALU.mult))
            node.store(tab_view, flat(tb))
            c.step(dve.tensor_tensor(X[:, :, :], X[:, :, :],
                                     rows[:, BIAS, :].unsqueeze(1).to_broadcast([P, W, D]), ALU.add))
        node_block(steps)
        project(ta, cheb_sb[:, 0, :], add_to_x)
        scaled = sb("scaled", [P, W, D])
        before, term = ta, tb
        for k in range(1, NCHEB):
            propagate(tab_dram, D, EW3, acc, False)
            to = term if k == 1 else before

            def steps(node, c, dve):
                c.step(dve.tensor_tensor(acc[:, :, :], acc[:, :, :], over_features(dis[:, :]), ALU.mult))
                if k == 1:
                    c.step(dve.tensor_scalar(to[:, :, :], acc[:, :, :], -1.0, None, ALU.mult))
                else:
                    c.step(dve.scalar_tensor_tensor(out=to[:, :, :], in0=acc[:, :, :], scalar=-2.0,
                                                    in1=to[:, :, :], op0=ALU.mult, op1=ALU.subtract))
                if k < NCHEB - 1:
                    c.step(dve.tensor_tensor(scaled[:, :, :], to[:, :, :], over_features(dis[:, :]), ALU.mult))
                    node.store(tab_view, flat(scaled))
            node_block(steps)
            project(to, cheb_sb[:, k, :], add_to_x)
            if k > 1:
                before, term = term, before

        with nc.Block() as block:
            @block.sync
            def _(sp):
                s_end = sem("output_stored")
                sp.dma_start(out[0:full].rearrange("(w p) f -> p w f", p=P), X[:, 0:W - 1, :]).then_inc(s_end, 16)
                sp.dma_start(out[full:N], X[0:TAIL, W - 1, :]).then_inc(s_end, 16)
                sp.wait_ge(s_end, 32)


_INS = ["x", "src", "dst", "edge_attr_40", "edge_weight", "node_type_119", "node_vec", "L0_gnn_w", "L0_gnn_b",
        "L1_gnn_W1", "L1_gnn_b1", "L1_gnn_W2", "L1_gnn_b2", "L1_gnn_emb", "L1_gnn_adaptW", "L1_gnn_gamma",
        "L1_gnn_beta", "L3_gnn_weight", "L3_gnn_bias"]


def kernel(**inputs):
    import numpy as _np
    import concourse.bacc as _bacc
    from concourse import mybir as _mybir
    from concourse.bass_utils import run_bass_kernel_spmd as _run

    nc = _bacc.Bacc("TRN2", target_bir_lowering=False, num_devices=1)
    arrays, args = {}, []
    for name in _INS:
        a = _np.ascontiguousarray(inputs[name])
        arrays[f"in_{name}"] = a
        args.append(nc.dram_tensor(f"in_{name}", a.shape, _mybir.dt.from_np(a.dtype), kind="ExternalInput").ap())
    shape = inputs["x"].shape
    args.append(nc.dram_tensor("out_0", shape, _mybir.dt.float32, kind="ExternalOutput").ap())
    gnn_kernel(nc, *args)
    r = _run(nc, [arrays], core_ids=[0])
    return r.results[0]["out_0"]
```

```python
from contextlib import ExitStack
from math import pi

import concourse.bass as bass
from concourse import mybir

F32, I32, BF16 = mybir.dt.float32, mybir.dt.int32, mybir.dt.bfloat16
ALU, ACT, AX = mybir.AluOpType, mybir.ActivationFunctionType, mybir.AxisListType
DVE_ENGINE, PE_ENGINE = mybir.EngineType.DVE, mybir.EngineType.PE

P = 128
RING = 5
K = 5
U = RING * K

EW, DREL, IDX, EW3, SWIN, SREL, DWIN, CW = range(8)
NF = 8
CUTOFF = 6.0
LN_EPS = 1e-5
OUT_OF_BOUNDS = 4.0e6


def ceil_div(a, b):
    return -(-a // b)


class Chain:

    def __init__(self, engine, sem, start=0):
        self.engine, self.sem, self.n = engine, sem, start

    def __call__(self, ins):
        ins.then_inc(self.sem, 1)
        self.n += 1
        return self

    def done(self):
        self.engine.wait_ge(self.sem, self.n)

    def step(self, ins):
        self(ins)
        self.done()


def lone_wait(engine, sem, value):
    engine.wait_ge(sem, value)
    engine.nop(nofuse=True)


def turns(engine, n, body):
    body(0, True)
    with engine.Fori(1, n) as i:
        body(i, False)


def gnn_kernel(nc, x, src, dst, edge_attr, edge_weight, node_type, node_vec, w0, b0, w1, b1, w2, b2,
               emb, adapt, gamma, beta, cheb, cheb_bias, out):
    N, D = x.shape
    E, R = edge_attr.shape
    NT, G = emb.shape
    NCHEB = cheb.shape[0]
    W = ceil_div(N, P)
    TAIL = N - (W - 1) * P
    EC = E // P
    ET = EC // U
    QC = ceil_div(E + W * (P - 1), P * U) * U
    QT = QC // U
    SB = 4
    SR = 2 * RING
    SG = ceil_div(ceil_div(E + W * (SB * P - 1), SB * P), SR) * SR
    ST = SG // SR
    SROWS = SG * SB * P
    REC = R + NF
    MSG = D + 4
    TOT, DEG, MREL = D, D + 1, D + 2
    AC = D + 2
    T0 = D + G
    HV = D + G + 1
    assert E == ET * P * U and R + NF == 48 and NF == 8 and W <= P and K * W <= 512

    ctx = ExitStack()

    def scoped(stack, name, shape, dt):
        return stack.enter_context(nc.sbuf_tensor(name, shape, dt))

    def sb(name, shape, dt=F32):
        return scoped(ctx, name, shape, dt)

    def sem(name):
        return ctx.enter_context(nc.semaphore(name))

    def sems(name):
        return [sem(f"{name}{g}") for g in range(RING)]

    rec_dram = nc.dram_tensor("records_by_dst", [QC * P, REC], F32).ap()
    PAD = ceil_div(SROWS // P, ET)
    msg_dram = nc.dram_tensor("messages_by_src", [P * PAD * ET, MSG], F32).ap()
    pad_view = msg_dram.rearrange("(p n) f -> p (n f)", p=P)
    u_dram = nc.dram_tensor("src_embedding_of_edges", [P, QC * G], F32).ap()
    tab0_dram = nc.dram_tensor("table_first", [P * W, T0], F32).ap()
    tab_dram = nc.dram_tensor("table", [P * W, D], F32).ap()
    types_dram = nc.dram_tensor("table_types", [NT, 2 * G], F32).ap()

    with ctx:
        win_d = sb("win_d", [1, QC], I32)
        win_s = sb("win_s", [1, SG], I32)
        ident = sb("ident", [P, P])
        iota = sb("iota", [P, P])
        iota_b = sb("iota_b", [P, P], BF16)
        lt_b = sb("lt_b", [P, P], BF16)
        ge_b = sb("ge_b", [P, P], BF16)
        ones_b = sb("ones_b", [P, P], BF16)
        ones_f = sb("ones_f", [P, P])
        w0_sb = sb("w0_sb", [D, D])
        w1t = sb("w1t", [2 * REC, 2 * D])
        w2t = sb("w2t", [2 * D + 1, 2 * D])
        cheb_sb = sb("cheb_sb", [D, NCHEB, D])
        b1_col = sb("b1_col", [2 * D, 1])
        rows = sb("rows", [P, 4, D])
        B0, GAMMA, BETA, BIAS = range(4)
        run_d = sb("run_d", [P, W])
        run_s = sb("run_s", [P, W])
        onehot_w = sb("onehot_w", [P, RING, K, W], BF16)
        rank = sb("rank", [P, K, W])
        mean = sb("mean", [P, W])
        var = sb("var", [P, W])
        mult = sb("mult", [P, W])
        dis = sb("dis", [P, W])
        half_pi = sb("half_pi", [P, 1])
        types_i = sb("types_i", [P, W], I32)

        s_pad = sem("padding_messages")
        v = sem("v")
        vn = [0]

        mark = {}

        def chain(engine):
            c = Chain(engine, v, vn[0])
            return c

        def keep(c):
            vn[0] = c.n

        edges = ExitStack()
        emeta = scoped(edges, "emeta", [P, EC, NF], F32)
        with ExitStack() as s0:
            def tmp(name, shape, dt=F32):
                return scoped(s0, name, shape, dt)

            src_i = tmp("src_i", [P, EC], I32)
            dst_i = tmp("dst_i", [P, EC], I32)
            t_i = tmp("t_i", [P, EC], I32)
            wf, wf2 = src_i[:, :].bitcast(F32), dst_i[:, :].bitcast(F32)
            junk_v = t_i[:, :].bitcast(F32)
            pcol = tmp("pcol", [P, 1])
            ge_d = tmp("ge_d", [P, W])
            ge_s = tmp("ge_s", [P, W])
            near = tmp("near", [P, W])
            cnt = tmp("cnt", [P, 2, W + 1])
            cnt_i = tmp("cnt_i", [P, 2, W], I32)
            nb = tmp("nb", [P, 2, W])
            inc = tmp("inc", [P, 2, W])
            begin = tmp("begin", [P, 2, W])
            begin_col = tmp("begin_col", [P, 2])
            sel = tmp("sel", [P, W])
            cols = tmp("cols", [P, 512])
            started = tmp("started", [P, 512], BF16)
            w_rows = tmp("w_rows", [D, 2, D])
            w1_one = tmp("w1_one", [R, D])
            w2_one = tmp("w2_one", [D, D])
            emb_sb = tmp("emb_sb", [P, G])
            adapt_sb = tmp("adapt_sb", [G, G])
            adapt_t = tmp("adapt_t", [G, G])
            emb_t = tmp("emb_t", [G, P])
            two = tmp("two", [P, 2 * G])
            types_w = tmp("types_w", [P, P], I32)
            nodes_w = tmp("nodes_w", [P, 2, P])
            fill = tmp("fill", [P, 25, REC])

            s_in, s_edge, s_fill, s_out = (sem(f"s0_{n}") for n in ("in", "edge", "fill", "out"))
            s_iota, s_pe, s_act, s_hist, s_uv, s_ready, s_ge = (
                sem(f"s0_{n}") for n in ("iota", "pe", "act", "hist", "uv", "ready", "ge"))
            ps = [s0.enter_context(nc.psum_tensor(f"ps0_{b}", [P, 512], F32)) for b in range(8)]
            NIN = 12 + 4 + 2
            full = (W - 1) * P
            with nc.Block() as block:
                @block.vector
                def _(dve):
                    c = chain(dve)
                    c(dve.memset(fill[:, :, :], 0.0))
                    c(dve.memset(types_w[:, :], 0))
                    c(dve.memset(nodes_w[:, :, :], 0.0))
                    c(dve.memset(emb_sb[:, :], 0.0))
                    c(dve.memset(w_rows[:, :, :], 0.0))
                    c(dve.memset(half_pi[:, :], pi / 2))
                    c(dve.memset(w1t[:, :], 0.0))
                    c(dve.memset(w2t[:, :], 0.0))
                    c(dve.memset(ones_b[:, :], 1.0))
                    c(dve.memset(ones_f[:, :], 1.0))
                    c(dve.memset(cnt[:, :, :], 0.0))
                    mark["zeroed"] = c.n
                    c.done()
                    for f in (DREL, SWIN, SREL):
                        c(dve.memset(fill[:, :, R + f:R + f + 1], -1.0))
                    mark["fill"] = c.n
                    dve.wait_ge(s_iota, 3)
                    c(dve.tensor_copy(iota_b[:, :], iota[:, :]))
                    c(dve.tensor_scalar(ident[:, :], iota[:, :], pcol[:, :], None, ALU.is_equal))
                    c(dve.tensor_scalar(lt_b[:, :], iota[:, :], pcol[:, :], None, ALU.is_gt))
                    c(dve.tensor_scalar(ge_b[:, :], iota[:, :], pcol[:, :], None, ALU.is_le))
                    c(dve.tensor_scalar(near[:, :], iota[:, 0:W], -1.0, 0.5, ALU.mult, ALU.add))
                    dve.wait_ge(s_edge, 32)
                    c(dve.tensor_tensor(emeta[:, :, EW3], src_i[:, :], dst_i[:, :], ALU.not_equal))
                    c.step(dve.tensor_scalar(t_i[:, :], src_i[:, :], P - 1, None, ALU.bitwise_and))
                    c.step(dve.tensor_copy(emeta[:, :, SREL], t_i[:, :]))
                    c.step(dve.tensor_scalar(t_i[:, :], src_i[:, :], 7, None, ALU.logical_shift_right))
                    c.step(dve.tensor_copy(emeta[:, :, SWIN], t_i[:, :]))
                    c.step(dve.scalar_tensor_tensor(out=emeta[:, :, IDX], in0=emeta[:, :, SREL], scalar=float(W),
                                                    in1=emeta[:, :, SWIN], op0=ALU.mult, op1=ALU.add))
                    c.step(dve.tensor_scalar(t_i[:, :], dst_i[:, :], P - 1, None, ALU.bitwise_and))
                    c.step(dve.tensor_copy(emeta[:, :, DREL], t_i[:, :]))
                    c.step(dve.tensor_scalar(t_i[:, :], dst_i[:, :], 7, None, ALU.logical_shift_right))
                    c.step(dve.tensor_copy(emeta[:, :, DWIN], t_i[:, :]))
                    mark["src used"] = c.n
                    dve.wait_ge(s_edge, 48)
                    c(dve.tensor_copy(emeta[:, :, EW], wf))
                    c.step(dve.tensor_scalar(t_i[:, :], wf, 0.5 / CUTOFF, None, ALU.mult))
                    c.step(dve.tensor_copy(wf2, t_i[:, :]))
                    c.step(dve.scalar_tensor_tensor(out=wf2, in0=wf2, scalar=-2 * CUTOFF, in1=wf,
                                                    op0=ALU.mult, op1=ALU.add))
                    c.step(dve.scalar_tensor_tensor(out=wf2, in0=wf2, scalar=-1.0, in1=wf2,
                                                    op0=ALU.mult, op1=ALU.max))
                    mark["remainder"] = c.n
                    dve.wait_ge(s_pe, 1)
                    c.step(dve.tensor_scalar(emeta[:, :, CW], emeta[:, :, CW], 0.5, 0.5, ALU.mult, ALU.add))
                    c.step(dve.scalar_tensor_tensor(out=emeta[:, :, CW], in0=wf, scalar=CUTOFF,
                                                    in1=emeta[:, :, CW], op0=ALU.is_lt, op1=ALU.mult))
                    keep(c)

                @block.sync
                def _(sp):
                    sp.dma_start(src_i[:, :], src.rearrange("(p n) -> p n", p=P)).then_inc(s_edge, 16)
                    sp.dma_start(dst_i[:, :], dst.rearrange("(p n) -> p n", p=P)).then_inc(s_edge, 16)
                    sp.wait_ge(v, mark["zeroed"])
                    loads = [
                        (types_w[0:W - 1, :], node_type[0:full].rearrange("(w p) -> w p", p=P)),
                        (types_w[W - 1:W, 0:TAIL], node_type[full:N].rearrange("(w p) -> w p", w=1)),
                        (nodes_w[0:W - 1, 1, :], node_vec[0:full].rearrange("(w p) -> w p", p=P)),
                        (nodes_w[W - 1:W, 1, 0:TAIL], node_vec[full:N].rearrange("(w p) -> w p", w=1)),
                        (w0_sb[:, :], w0), (w_rows[:, 0, 0:R], w1), (w_rows[:, 1, :], w2),
                        (cheb_sb[:, :, :], cheb.rearrange("k i o -> i k o")),
                        (b1_col[0:D, :], b1.rearrange("(p a) -> p a", a=1)),
                        (b1_col[D:2 * D, :], b1.rearrange("(p a) -> p a", a=1)),
                        (emb_sb[0:NT, :], emb), (adapt_sb[:, :], adapt),
                    ]
                    for to, of in loads:
                        sp.dma_start(to, of).then_inc(s_in, 16)
                    row = lambda a: a.rearrange("(a d) -> a d", a=1)
                    for k, a in enumerate((b0, gamma, beta, cheb_bias)):
                        sp.dma_start(rows[:, k, :], row(a).to_broadcast([P, D])).then_inc(s_in, 16)
                    for k in range(2):
                        sp.dma_start(w2t[2 * D:2 * D + 1, k * D:(k + 1) * D], row(b2)).then_inc(s_in, 16)
                    sp.wait_ge(v, mark["fill"])
                    per = QC // 25
                    view = rec_dram.rearrange("(p n) f -> p (n f)", p=P)
                    with sp.Fori(0, per) as n:
                        sp.dma_start(view[:, bass.ds(n * (25 * REC), 25 * REC)],
                                     fill[:, :, :].rearrange("p a b -> p (a b)")).then_inc(s_fill, 16)
                @block.gpsimd
                def _(pool):
                    pool.iota(iota[:, :], [[1, P]], base=0, channel_multiplier=0,
                              allow_small_or_imprecise_dtypes=True).then_inc(s_iota, 1)
                    pool.iota(pcol[:, :], [[0, 1]], base=0, channel_multiplier=1,
                              allow_small_or_imprecise_dtypes=True).then_inc(s_iota, 1)
                    pool.iota(cols[:, :], [[1, 512]], base=0, channel_multiplier=0,
                              allow_small_or_imprecise_dtypes=True).then_inc(s_iota, 1)

                @block.scalar
                def _(act):
                    act.wait_ge(v, mark["src used"])
                    act.dma_start(wf, edge_weight.rearrange("(p n) -> p n", p=P)).then_inc(s_edge, 16)
                    act.wait_ge(v, mark["remainder"])
                    act.activation(emeta[:, :, CW], wf2, ACT.Sin, bias=half_pi[:, :],
                                   scale=-pi / CUTOFF).then_inc(s_pe, 1)


            with nc.Block() as block:
                @block.vector
                def _(dve):
                    c = chain(dve)
                    dve.wait_ge(s_in, 16 * NIN)
                    c.step(dve.tensor_copy(nodes_w[:, 0, :], types_w[:, :]))
                    mark["types"] = c.n
                    c.step(dve.tensor_scalar(junk_v, emeta[:, :, DWIN], 0.0, None, ALU.is_ge, ALU.add,
                                             accum_out=ge_d[:, 0:1]))
                    keep(c)
                    with dve.Fori(1, W) as w:
                        dve.wait_ge(v, w + (c.n - 1))
                        dve.tensor_scalar(junk_v, emeta[:, :, DWIN], iota[:, bass.ds(w, 1)], None,
                                          ALU.is_ge, ALU.add, accum_out=ge_d[:, bass.ds(w, 1)]).then_inc(v, 1)
                    c.n += W - 1
                    c.done()
                    keep(c)

                @block.scalar
                def _(act):
                    act.activation(wf2, emeta[:, :, SWIN], ACT.Sign, bias=near[:, 0:1], scale=1.0,
                                   accum_out=ge_s[:, 0:1]).then_inc(s_ge, 1)
                    with act.Fori(1, W) as w:
                        act.wait_ge(s_ge, w)
                        act.activation(wf2, emeta[:, :, SWIN], ACT.Sign, bias=near[:, bass.ds(w, 1)],
                                       scale=1.0, accum_out=ge_s[:, bass.ds(w, 1)]).then_inc(s_ge, 1)
                    act.wait_ge(s_ge, W)

                @block.tensor
                def _(pe):
                    pe.wait_ge(v, mark["types"])
                    pe.transpose(ps[0][0:R, 0:D], w_rows[:, 0, 0:R], ident[0:D, 0:D])
                    pe.transpose(ps[1][0:D, 0:D], w_rows[:, 1, :], ident[0:D, 0:D])
                    pe.transpose(ps[2][0:G, 0:P], emb_sb[:, :], ident[:, :])
                    pe.transpose(ps[3][0:G, 0:G], adapt_sb[:, :], ident[0:G, 0:G])
                    for k in range(2):
                        last = pe.transpose(ps[4 + k][0:P, 0:W], nodes_w[0:W, k, :], ident[0:W, 0:W])
                    last.then_inc(s_ready, 1)

            with nc.Block() as block:
                @block.vector
                def _(dve):
                    c = chain(dve)
                    dve.wait_ge(s_ready, 1)
                    c(dve.tensor_copy(w1_one[:, :], ps[0][0:R, 0:D]))
                    c(dve.tensor_copy(w2_one[:, :], ps[1][0:D, 0:D]))
                    mark["weights"] = c.n
                    c(dve.tensor_copy(emb_t[:, :], ps[2][0:G, 0:P]))
                    c(dve.tensor_copy(adapt_t[:, :], ps[3][0:G, 0:G]))
                    c(dve.tensor_copy(types_i[:, :], ps[4][:, 0:W]))
                    c(dve.tensor_copy(mult[:, :], ps[5][:, 0:W]))
                    c(dve.tensor_scalar(ge_s[:, :], ge_s[:, :], float(EC), 0.5, ALU.add, ALU.mult))
                    c(dve.tensor_copy(two[:, 0:G], emb_sb[:, :]))
                    mark["transposed"] = c.n
                    dve.wait_ge(s_pe, 2)
                    c.step(dve.tensor_copy(two[:, G:2 * G], ps[6][:, 0:G]))
                    mark["two"] = c.n
                    c(dve.tensor_copy(cnt[:, 0, 0:W], ps[7][:, 0:W]))
                    c.step(dve.tensor_copy(cnt[:, 1, 0:W], ps[7][:, 256:256 + W]))
                    c.step(dve.tensor_tensor(nb[:, :, :], cnt[:, :, 0:W], cnt[:, :, 1:W + 1], ALU.subtract))
                    c(dve.tensor_scalar(cnt_i[:, 0, :], nb[:, 0, :], float(P - 1), None, ALU.add))
                    c.step(dve.tensor_scalar(cnt_i[:, 1, :], nb[:, 1, :], float(SB * P - 1), None, ALU.add))
                    c(dve.tensor_scalar(cnt_i[:, 0, :], cnt_i[:, 0, :], P.bit_length() - 1, None, ALU.logical_shift_right))
                    c.step(dve.tensor_scalar(cnt_i[:, 1, :], cnt_i[:, 1, :], (SB * P).bit_length() - 1, None,
                                             ALU.logical_shift_right))
                    c.step(dve.tensor_copy(nb[:, :, :], cnt_i[:, :, :]))
                    for k in range(2):
                        c(dve.tensor_tensor_scan(inc[:, k, :], ones_f[:, 0:W], nb[:, k, :], 0.0, ALU.mult, ALU.add))
                    c.done()
                    c.step(dve.tensor_tensor(begin[:, :, :], inc[:, :, :], nb[:, :, :], ALU.subtract))
                    c(dve.tensor_scalar(run_d[:, :], begin[:, 0, :], float(P), None, ALU.mult))
                    c(dve.tensor_scalar(run_s[:, :], begin[:, 1, :], float(SB * P), None, ALU.mult))
                    for k in range(2):
                        c.step(dve.tensor_tensor(sel[0:W, :], begin[0:W, k, :], ident[0:W, 0:W], ALU.mult))
                        c.step(dve.tensor_reduce(begin_col[0:W, k:k + 1], sel[0:W, :], AX.X, ALU.add))
                    n = 0
                    for k, (row, count) in enumerate(((win_d, QC), (win_s, SG))):
                        for a in range(0, count, 512):
                            m = min(512, count - a)
                            c.step(dve.tensor_scalar(sel[0:W, 0:1], begin_col[0:W, k:k + 1], float(-a), None, ALU.add))
                            c.step(dve.tensor_scalar(started[0:W, 0:m], cols[0:W, 0:m], sel[0:W, 0:1], None, ALU.is_ge))
                            mark["started", n] = c.n
                            dve.wait_ge(s_uv, 1 + n)
                            c.step(dve.tensor_scalar(row[:, a:a + m], ps[0][0:1, 0:m], -1.0, None, ALU.add))
                            n += 1
                    keep(c)

                @block.sync
                def _(sp):
                    sp.wait_ge(v, mark["two"])
                    sp.dma_start(types_dram, two[0:NT, :]).then_inc(s_out, 16)
                    for k in range(2):
                        sp.dma_start(w1t[k * REC:k * REC + R, k * D:(k + 1) * D], w1_one[:, :]).then_inc(s_out, 16)
                        sp.dma_start(w2t[k * D:(k + 1) * D, k * D:(k + 1) * D], w2_one[:, :]).then_inc(s_out, 16)
                    sp.wait_ge(s_out, 16 * 5)
                    sp.wait_ge(s_fill, 16 * (QC // 25))

                @block.tensor
                def _(pe):
                    pe.wait_ge(v, mark["transposed"])
                    pe.matmul(ps[6][:, 0:G], emb_t[:, :], adapt_t[:, :], start=True, stop=True)
                    pe.matmul(ps[7][:, 0:W], ones_f[:, :], ge_d[:, :], start=True, stop=True)
                    pe.matmul(ps[7][:, 256:256 + W], ones_f[:, :], ge_s[:, :], start=True, stop=True).then_inc(s_pe, 1)
                    n = 0
                    for count in (QC, SG):
                        for a in range(0, count, 512):
                            m = min(512, count - a)
                            pe.wait_ge(v, mark["started", n])
                            pe.matmul(ps[0][0:1, 0:m], ones_b[0:W, 0:1], started[0:W, 0:m],
                                      start=True, stop=True).then_inc(s_uv, 1)
                            n += 1

        def rank_start(pe, free, first_row):
            pe.matmul(free, ones_f[0:1, :], first_row.unsqueeze(1).to_broadcast([1, K, W]),
                      start=True, stop=True, skip_group_check=True)

        def rank_before(pe, free, onehot):
            last = pe.matmul(free, lt_b[:, :], onehot, start=False, stop=True, skip_group_check=True)
            for j in range(K - 1):
                last = pe.matmul(free[:, j + 1:K, :], ones_b[:, :],
                                 onehot[:, j:j + 1, :].to_broadcast([P, K - 1 - j, W]),
                                 start=False, stop=True, skip_group_check=True)
            return last

        def rank_rest(pe, free, onehot):
            pe.matmul(free, ge_b[:, :], onehot, start=False, stop=True, skip_group_check=True)
            for j in range(1, K):
                pe.matmul(free[:, 0:j, :], ones_b[:, :], onehot[:, j:j + 1, :].to_broadcast([P, j, W]),
                          start=False, stop=True, skip_group_check=True)

        with ExitStack() as s1:
            recb = scoped(s1, "recb", [P, RING, K, REC], F32)
            row_i = scoped(s1, "row_i", [P, RING, K], I32)
            ps_free = s1.enter_context(nc.psum_tensor("ps1_free", [P, 512], F32))
            free = ps_free[:, 0:K * W].rearrange("p (k w) -> p k w", k=K)
            fill_msg = scoped(s1, "fill_msg", [P, PAD, MSG], F32)
            ld, put = sems("s1_attr"), sems("s1_put")
            meta, oh, rk = (sem(f"s1_{n}") for n in ("meta", "onehot", "rank"))
            attr = edge_attr.rearrange("(p n) f -> p n f", p=P)
            with nc.Block() as block:
                @block.vector
                def _(dve):
                    c = chain(dve)
                    c.step(dve.memset(fill_msg[:, :, :], 0.0))
                    c.step(dve.memset(fill_msg[:, :, MREL:MREL + 1], -1.0))
                    keep(c)
            base_v = vn[0]

            with nc.Block() as block:
                @block.sync
                def _(sp):
                    def turn(i, first):
                        for g in range(RING):
                            if not first:
                                sp.wait_ge(put[g], i * (16 * K))
                            sp.dma_start(recb[:, g, :, 0:R],
                                         attr[:, bass.ds(i * U + g * K, K), :]).then_inc(ld[g], 16)
                        sp.dma_start(pad_view[:, bass.ds(i * (PAD * MSG), PAD * MSG)],
                                     fill_msg[:, :, :].rearrange("p a b -> p (a b)")).then_inc(s_pad, 16)
                    turns(sp, ET, turn)
                    sp.wait_ge(s_pad, 16 * ET)

                @block.scalar
                def _(act):
                    def turn(i, first):
                        for g in range(RING):
                            if not first:
                                act.wait_ge(put[g], i * (16 * K))
                            act.copy(recb[:, g, :, R:REC],
                                     emeta[:, bass.ds(i * U + g * K, K), :]).then_inc(meta, 1)
                    turns(act, ET, turn)

                @block.vector
                def _(dve):
                    c = chain(dve)
                    base = base_v

                    def finish(i, g):
                        dve.wait_ge(rk, i * RING + (g + 1))
                        rank_dve_steps(i, g)

                    def rank_dve_steps(i, g):
                        at = lambda k: i * (2 * RING) + (base + 2 * g + k)
                        dve.wait_ge(v, at(0))
                        dve.tensor_tensor(rank[:, :, :], free, onehot_w[:, g, :, :], ALU.mult).then_inc(v, 1)
                        dve.wait_ge(v, at(1))
                        with nc.allow_low_precision(reason="row numbers: whole, below 2^24"):
                            dve.tensor_reduce(row_i[:, g, :], rank[:, :, :], AX.X, ALU.add).then_inc(v, 1)

                    def turn(i, first):
                        for g in range(RING):
                            dve.wait_ge(meta, i * RING + (g + 1))
                            for k in range(K):
                                last = dve.tensor_scalar(onehot_w[:, g, k, :], iota_b[:, 0:W],
                                                         recb[:, g, k, R + DWIN:R + DWIN + 1], None, ALU.is_equal)
                            last.then_inc(oh, 1)
                            if g:
                                finish(i, g - 1)
                            elif not first:
                                finish(i - 1, RING - 1)
                    turns(dve, ET, turn)
                    finish(ET - 1, RING - 1)
                    c.n = base + 2 * RING * ET
                    keep(c)

                @block.tensor
                def _(pe):
                    rank_start(pe, free, run_d[0:1, :])

                    def turn(i, first):
                        for g in range(RING):
                            pe.wait_ge(oh, i * RING + (g + 1))
                            if g or not first:
                                lone_wait(pe, v, i * (2 * RING) + (base_v + 2 * g - 1))
                                rank_rest(pe, free, onehot_w[:, (g - 1) % RING, :, :])
                            rank_before(pe, free, onehot_w[:, g, :, :]).then_inc(rk, 1)
                    turns(pe, ET, turn)

                @block.gpsimd
                def _(pool):
                    def turn(i, first):
                        for g in range(RING):
                            lone_wait(pool, v, i * (2 * RING) + (base_v + 2 * g + 2))
                            lone_wait(pool, ld[g], i * 16 + 16)
                            for k in range(K):
                                pool.indirect_dma_start(
                                    rec_dram, bass.IndirectOffsetOnAxis(ap=row_i[:, g, k:k + 1], axis=0),
                                    recb[:, g, k, :], None).then_inc(put[g], 16)
                    turns(pool, ET, turn)
                    for g in range(RING):
                        pool.wait_ge(put[g], ET * 16 * K)
        edges.close()

        X = sb("X", [P, W, D])
        s_node = sem("node_act")
        s_dma = sem("node_dma")
        n_node, n_dma = [0], [0]

        def over_features(a):
            return a.unsqueeze(2).to_broadcast([P, W, D])

        class Node:

            def __init__(self, dve):
                self.dve, self.c, self.acts, self.stores = dve, chain(dve), [], []

            def sqrt(self, a):
                self.acts.append((self.c.n, a, n_node[0]))
                n_node[0] += 1
                self.dve.wait_ge(s_node, n_node[0])

            def store(self, to, of):
                self.stores.append((self.c.n, to, of))
                n_dma[0] += 16

            def layernorm(self, to, of, square, relu):
                c, dve = self.c, self.dve
                c.step(dve.tensor_reduce(mean[:, :], of, AX.X, ALU.add))
                c.step(dve.tensor_scalar(mean[:, :], mean[:, :], 1.0 / D, None, ALU.mult))
                c.step(dve.tensor_tensor(to, of, over_features(mean[:, :]), ALU.subtract))
                c.step(dve.tensor_tensor(square, to, to, ALU.mult))
                c.step(dve.tensor_reduce(var[:, :], square, AX.X, ALU.add))
                c.step(dve.tensor_scalar(var[:, :], var[:, :], 1.0 / D, LN_EPS, ALU.mult, ALU.add))
                self.sqrt(var[:, :])
                c.step(dve.reciprocal(var[:, :], var[:, :]))
                c.step(dve.tensor_tensor(to, to, over_features(var[:, :]), ALU.mult))
                if relu:
                    c.step(dve.tensor_scalar(to, to, 0.0, None, ALU.max))

        def node_block(steps, pool_steps=None, before=()):
            with nc.Block() as block:
                node = []

                @block.vector
                def _(dve):
                    node.append(Node(dve))
                    if before:
                        n_dma[0] += 16 * len(before)
                        dve.wait_ge(s_dma, n_dma[0])
                    steps(node[0], node[0].c, dve)
                    keep(node[0].c)

                @block.scalar
                def _(act):
                    for at, a, _ in node[0].acts:
                        act.wait_ge(v, at)
                        act.activation(a, a, ACT.Sqrt).then_inc(s_node, 1)

                @block.sync
                def _(sp):
                    for to, of in before:
                        sp.dma_start(to, of).then_inc(s_dma, 16)
                    for at, to, of in node[0].stores:
                        sp.wait_ge(v, at)
                        sp.dma_start(to, of).then_inc(s_dma, 16)
                    if before or node[0].stores:
                        sp.wait_ge(s_dma, n_dma[0])

                if pool_steps is not None:
                    @block.gpsimd
                    def _(pool):
                        pool_steps(pool)

        PW = 7
        PT = W // (2 * PW)
        assert W == 2 * PW * PT
        pj = {n: [sem(f"pj_{n}{s}") for s in range(2)] for n in ("stage", "trans", "lhs", "prod", "out")}
        n_pj = [0]

        def project(rows_of, matrix, put):
            base = PT * n_pj[0]
            n_pj[0] += 1
            with ExitStack() as s:
                stage = scoped(s, f"stage{n_pj[0]}", [P, 2, PW, D], F32)
                lhs = scoped(s, f"lhs{n_pj[0]}", [D, 2, PW * P], F32)
                pst = s.enter_context(nc.psum_tensor(f"pst{n_pj[0]}", [P, 2, 1024], F32))
                pso = s.enter_context(nc.psum_tensor(f"pso{n_pj[0]}", [P, 2, 512], F32))
                with nc.Block() as block:
                    @block.scalar
                    def _(act):
                        def turn(i, first):
                            for q in range(2):
                                if not first:
                                    act.wait_ge(pj["trans"][q], i + base)
                                act.copy(stage[:, q, :, :], rows_of[:, bass.ds((i * 2 + q) * PW, PW), :]
                                         ).then_inc(pj["stage"][q], 1)
                                act.wait_ge(pj["trans"][q], i + (base + 1))
                                if not first:
                                    act.wait_ge(pj["prod"][q], i + base)
                                act.copy(lhs[:, q, :], pst[0:D, q, 0:PW * P]).then_inc(pj["lhs"][q], 1)
                        turns(act, PT, turn)

                    @block.tensor
                    def _(pe):
                        def turn(i, first):
                            for q in range(2):
                                pe.wait_ge(pj["stage"][q], i + (base + 1))
                                if not first:
                                    lone_wait(pe, pj["lhs"][q], i + base)
                                for n in range(PW):
                                    last = pe.transpose(pst[0:D, q, n * P:(n + 1) * P], stage[:, q, n, :],
                                                        ident[:, :])
                                last.then_inc(pj["trans"][q], 1)
                                pe.wait_ge(pj["lhs"][q], i + (base + 1))
                                if not first:
                                    pe.wait_ge(pj["out"][q], i + base)
                                for n in range(PW):
                                    last = pe.matmul(pso[:, q, n * D:(n + 1) * D],
                                                     lhs[:, q, n * P:(n + 1) * P], matrix,
                                                     start=True, stop=True)
                                last.then_inc(pj["prod"][q], 1)
                        turns(pe, PT, turn)

                    @block.vector
                    def _(dve):
                        def turn(i, first):
                            for q in range(2):
                                dve.wait_ge(pj["prod"][q], i + (base + 1))
                                put(dve, pso[:, q, 0:PW * D].rearrange("p (w f) -> p w f", w=PW),
                                    (i * 2 + q) * PW).then_inc(pj["out"][q], 1)
                        turns(dve, PT, turn)

        full = (W - 1) * P
        meta = sb("meta", [P, QC, 4])
        hv_scope = ExitStack()
        hv = scoped(hv_scope, "hv", [P, W, HV], F32)
        with ExitStack() as s2:
            tab0 = scoped(s2, "tab0", [P, W, T0], F32)
            h = scoped(s2, "h0", [P, W, D], F32)
            spare = meta[:, :, :].rearrange("p n f -> p (n f)")
            square = spare[:, 0:W * D].rearrange("p (w f) -> p w f", w=W)
            uv = spare[:, W * D:W * (D + 2 * G)].rearrange("p (w f) -> p w f", w=W)
            s_x0, s_uvg = sem("x_zeroed"), sem("types_gathered")

            with nc.Block() as block:
                @block.vector
                def _(dve):
                    dve.memset(X[:, :, :], 0.0).then_inc(s_x0, 1)

            def types_of_nodes(pool):
                for w in range(W):
                    pool.indirect_dma_start(
                        uv[:, w, :], None, types_dram,
                        bass.IndirectOffsetOnAxis(ap=types_i[:, w:w + 1], axis=0)).then_inc(s_uvg, 16)
                pool.wait_ge(s_uvg, 16 * W)

            def steps(node, c, dve):
                node.layernorm(h[:, :, :], X[:, :, :], square[:, :, :], True)
                dve.wait_ge(s_uvg, 16 * W)
                c(dve.tensor_copy(tab0[:, :, D:T0], uv[:, :, 0:G]))
                c(dve.tensor_copy(hv[:, :, D:D + G], uv[:, :, G:2 * G]))
                c(dve.tensor_copy(hv[:, :, D + G], mult[:, :]))
                c.done()

            node_block(steps, types_of_nodes,
                       before=[(X[:, 0:W - 1, :], x[0:full].rearrange("(w p) f -> p w f", p=P)),
                               (X[0:TAIL, W - 1, :], x[full:N])])
            project(h, w0_sb[:, :], lambda dve, of, w: dve.tensor_copy(tab0[:, bass.ds(w, PW), 0:D], of))
            node_block(lambda node, c, dve: node.store(
                tab0_dram.rearrange("(p w) f -> p (w f)", p=P), tab0[:, :, :].rearrange("p w f -> p (w f)")))

        rows_scope = ExitStack()
        src_row = scoped(rows_scope, "src_row", [P, QC], I32)
        pg_dma = sems("prop_gather")
        pg_st, pg_oh, pg_mm = (sem(f"prop_{n}") for n in ("staged", "onehot", "sum"))
        n_prop = [0]

        def windows(engine_type, row, at, count):
            return nc.values_load_multi_w_load_instructions(
                row[0:1, bass.ds(at, count)], engines=(engine_type,), min_val=0, max_val=W - 1,
                skip_runtime_bounds_check_because="windows are counted below W")[1]

        def propagate(table, width, weight, acc, first_layer):
            n = n_prop[0]
            n_prop[0] += 1
            base = n * QT
            per = K + (3 if first_layer else 0)
            with ExitStack() as s:
                gath = scoped(s, f"gath{n}", [P, RING, K, width], F32)
                onehot = scoped(s, f"onehot{n}", [P, RING, K, P], F32)
                idx_s = scoped(s, f"idx_s{n}", [P, RING, K], I32)
                fields = scoped(s, f"fields{n}", [P, RING, K, NF if first_layer else 4], F32)
                sums = s.enter_context(nc.psum_tensor(f"sums{n}", [P, RING, 512], F32))
                acc_flat = acc[:, :, :].rearrange("p w f -> p (w f)")
                if first_layer:
                    pad = scoped(s, "pad", [P, K], F32)
                    rank_sum = scoped(s, "rank_sum", [P, K], F32)
                    ps_free = s.enter_context(nc.psum_tensor("free_src", [P, 512], F32))
                    free = ps_free[:, 0:K * W].rearrange("p (k w) -> p k w", k=K)
                    ld, us = sems("fields_load"), sems("types_save")
                    woh, rk = sem("windows_onehot"), sem("windows_rank")
                    u_view = u_dram.rearrange("p (n f) -> p n f", f=G)
                    rec_view = rec_dram.rearrange("(n p) f -> p n f", p=P)

                def sum_of(g):
                    return sums[:, g, 0:K * D]

                with nc.Block() as block:
                    @block.vector
                    def _(dve):
                        c = chain(dve)
                        c.step(dve.memset(acc_flat, 0.0))
                        keep(c)
                    mark["prop"] = vn[0]
                b_v = vn[0]

                def v_at(i, g, k):
                    return i * (per * RING) + (b_v + per * g + k)

                with nc.Block() as block:
                    if first_layer:
                        @block.sync
                        def _(sp):
                            def load(i, g):
                                sp.dma_start(fields[:, g, :, :],
                                             rec_view[:, bass.ds(i * U + g * K, K), R:REC]).then_inc(ld[g], 16)

                            def load_next(i, g):
                                lone_wait(sp, v, v_at(i, g, per))
                                lone_wait(sp, pg_st, (i + 1) * RING + (base * RING + g + 1 - RING))
                                load(i + 1, g)

                            def turn(i, first, last):
                                for g in range(RING):
                                    lone_wait(sp, pg_dma[g], (i + (base + 1)) * (16 * K))
                                    sp.dma_start(u_view[:, bass.ds(i * U + g * K, K), :],
                                                 gath[:, g, :, D:T0]).then_inc(us[g], 16)
                                    if g and not last:
                                        load_next(i, g - 1)
                                    elif g == 0 and not first:
                                        load_next(i - 1, RING - 1)
                            for g in range(RING):
                                load(0, g)
                            turn(0, True, False)
                            with sp.Fori(1, QT - 1) as i:
                                turn(i, False, False)
                            turn(QT - 1, False, True)
                            for g in range(RING):
                                sp.wait_ge(us[g], 16 * QT)

                    @block.scalar
                    def _(act):
                        def turn(i, first):
                            for g in range(RING):
                                at = bass.ds(i * U + g * K, K)
                                if not first:
                                    act.wait_ge(pg_dma[g], (i + base) * (16 * K))
                                if first_layer:
                                    act.wait_ge(ld[g], i * 16 + 16)
                                    act.copy(meta[:, at, :], fields[:, g, :, 0:4])
                                    act.copy(idx_s[:, g, :], fields[:, g, :, IDX]).then_inc(pg_st, 1)
                                else:
                                    if not first:
                                        act.wait_ge(pg_oh, i * RING + (base * RING + g + 1 - RING))
                                    act.copy(fields[:, g, :, :], meta[:, at, :])
                                    act.copy(idx_s[:, g, :], meta[:, at, IDX]).then_inc(pg_st, 1)
                        turns(act, QT, turn)

                    @block.gpsimd
                    def _(pool):
                        def turn(i, first):
                            for g in range(RING):
                                lone_wait(pool, pg_st, i * RING + (base * RING + g + 1))
                                if not first:
                                    lone_wait(pool, pg_mm, i * RING + (base * RING + g + 1 - RING))
                                    if first_layer:
                                        lone_wait(pool, us[g], i * 16)
                                for k in range(K):
                                    pool.indirect_dma_start(
                                        gath[:, g, k, :], None, table,
                                        bass.IndirectOffsetOnAxis(ap=idx_s[:, g, k:k + 1], axis=0)
                                    ).then_inc(pg_dma[g], 16)
                        turns(pool, QT, turn)

                    @block.vector
                    def _(dve):
                        def finish(i, g):
                            ws = windows(DVE_ENGINE, win_d, i * U + g * K, K)
                            n = 0
                            if first_layer:
                                n = per - K
                                dve.wait_ge(rk, i * RING + (g + 1))
                                dve.wait_ge(v, v_at(i, g, 0))
                                dve.tensor_tensor(rank[:, :, :], free, onehot_w[:, g, :, :], ALU.mult).then_inc(v, 1)
                                dve.tensor_scalar(pad[:, :], fields[:, g, :, SWIN], 0.0, OUT_OF_BOUNDS,
                                                  ALU.is_lt, ALU.mult)
                                dve.wait_ge(v, v_at(i, g, 1))
                                dve.tensor_reduce(rank_sum[:, :], rank[:, :, :], AX.X, ALU.add).then_inc(v, 1)
                                dve.wait_ge(v, v_at(i, g, 2))
                                dve.tensor_tensor(src_row[:, bass.ds(i * U + g * K, K)], rank_sum[:, :], pad[:, :],
                                                  ALU.add).then_inc(v, 1)
                            dve.wait_ge(pg_mm, i * RING + (base * RING + g + 1))
                            for k in range(K):
                                to = acc_flat[:, bass.ds(ws[k] * D, D)]
                                dve.wait_ge(v, v_at(i, g, n + k))
                                dve.tensor_tensor(to, to, sum_of(g)[:, k * D:(k + 1) * D], ALU.add).then_inc(v, 1)

                        def turn(i, first):
                            for g in range(RING):
                                if first_layer:
                                    dve.wait_ge(ld[g], i * 16 + 16)
                                else:
                                    dve.wait_ge(pg_st, i * RING + (base * RING + g + 1))
                                if not first:
                                    dve.wait_ge(pg_mm, i * RING + (base * RING + g + 1 - RING))
                                f = fields[:, g, :, :]
                                for k in range(K):
                                    last = dve.tensor_scalar(onehot[:, g, k, :], iota[:, :], f[:, k, DREL:DREL + 1],
                                                             f[:, k, weight:weight + 1], ALU.is_equal, ALU.mult)
                                last.then_inc(pg_oh, 1)
                                if first_layer:
                                    for k in range(K):
                                        last = dve.tensor_scalar(onehot_w[:, g, k, :], iota_b[:, 0:W],
                                                                 f[:, k, SWIN:SWIN + 1], None, ALU.is_equal)
                                    last.then_inc(woh, 1)
                                if g:
                                    finish(i, g - 1)
                                elif not first:
                                    finish(i - 1, RING - 1)
                        turns(dve, QT, turn)
                        finish(QT - 1, RING - 1)
                        vn[0] = b_v + per * RING * QT

                    @block.tensor
                    def _(pe):
                        if first_layer:
                            rank_start(pe, free, run_s[0:1, :])

                        def turn(i, first):
                            for g in range(RING):
                                if first_layer:
                                    pe.wait_ge(woh, i * RING + (g + 1))
                                    if g or not first:
                                        lone_wait(pe, v, v_at(i, g, 1 - per))
                                        rank_rest(pe, free, onehot_w[:, (g - 1) % RING, :, :])
                                    rank_before(pe, free, onehot_w[:, g, :, :]).then_inc(rk, 1)
                                pe.wait_ge(pg_oh, i * RING + (base * RING + g + 1))
                                pe.wait_ge(pg_dma[g], (i + (base + 1)) * (16 * K))
                                if not first:
                                    pe.wait_ge(v, v_at(i - 1, g, per))
                                for k in range(K):
                                    last = pe.matmul(sum_of(g)[:, k * D:(k + 1) * D], onehot[:, g, k, :],
                                                     gath[:, g, k, 0:D], start=True, stop=True)
                                last.then_inc(pg_mm, 1)
                        turns(pe, QT, turn)

        with ExitStack() as s3:
            acc = scoped(s3, "acc0", [P, W, D], F32)
            square = acc
            propagate(tab0_dram, T0, EW, acc, True)

            def steps(node, c, dve):
                c.step(dve.tensor_tensor(acc[:, :, :], acc[:, :, :],
                                         rows[:, B0, :].unsqueeze(1).to_broadcast([P, W, D]), ALU.add))
                c.step(dve.scalar_tensor_tensor(out=X[:, :, :], in0=acc[:, :, :], scalar=0.0, in1=X[:, :, :],
                                                op0=ALU.max, op1=ALU.add))
                node.layernorm(hv[:, :, 0:D], X[:, :, :], square[:, :, :], True)

            node_block(steps)

        with ExitStack() as s4:
            recl = scoped(s4, "recl", [P, RING, K, REC], F32)
            ul = scoped(s4, "ul", [P, RING, K, G], F32)
            row_s = scoped(s4, "row_s", [P, RING, K], I32)
            oh_b = scoped(s4, "oh_b", [P, RING, K, P], BF16)
            oht = scoped(s4, "oht", [P, RING, K, P], F32)
            ident_b = scoped(s4, "ident_b", [P, P], BF16)
            PAIRS = ceil_div(K, 2)
            attr_t = scoped(s4, "attr_t", [2 * REC, RING, PAIRS * P], F32)
            act1 = scoped(s4, "act1", [2 * D + 1, RING, PAIRS * P], F32)
            msgs = scoped(s4, "msgs", [P, RING, K, MSG], F32)
            uxv = scoped(s4, "uxv", [P, K, G], F32)
            logit = scoped(s4, "logit", [P, K], F32)
            scale = scoped(s4, "scale", [P, K], F32)
            gate_s = scoped(s4, "gate_s", [P, K, D], F32)
            ps_oht = s4.enter_context(nc.psum_tensor("ps_oht", [P, K * P], BF16))
            ps_at = s4.enter_context(nc.psum_tensor("ps_at", [P, 512], F32))
            ps_h1 = s4.enter_context(nc.psum_tensor("ps_h1", [P, 512], F32))
            ps_gate = s4.enter_context(nc.psum_tensor("ps_gate", [P, 512], F32))
            ps_hv = s4.enter_context(nc.psum_tensor("ps_hv", [P, 2, 512], F32))
            ld, ldu, put = sems("l1_load"), sems("l1_types"), sems("l1_put")
            ohb, tr, cp, st, h1s, si, hvs, gt = (
                sem(f"l1_{n}") for n in ("onehot", "trans", "copied", "staged", "hidden", "silu", "dstrow", "gate"))
            hv_flat = hv[:, :, :].rearrange("p w f -> p (w f)")
            rec_view = rec_dram.rearrange("(n p) f -> p n f", p=P)
            u_view = u_dram.rearrange("p (n f) -> p n f", f=G)

            with nc.Block() as block:
                @block.vector
                def _(dve):
                    c = chain(dve)
                    c(dve.memset(msgs[:, :, :, :].rearrange("p a b f -> p (a b f)"), 0.0))
                    c(dve.memset(act1[:, :, :], 1.0))
                    c(dve.memset(ps_at[:, :], 0.0))
                    c(dve.tensor_copy(ident_b[:, :], ident[:, :]))
                    c.done()
                    keep(c)

            b_v = vn[0]
            per = 6

            def v_at(i, g, k):
                return i * (per * RING) + (b_v + per * g + k)

            with nc.Block() as block:
                @block.sync
                def _(sp):
                    def turn(i, first):
                        for g in range(RING):
                            if not first:
                                lone_wait(sp, v, v_at(i - 1, g, per))
                                lone_wait(sp, st, i * RING + (g + 1 - RING))
                                lone_wait(sp, tr, i * RING + (g + 1 - RING))
                            at = bass.ds(i * U + g * K, K)
                            sp.dma_start(recl[:, g, :, :], rec_view[:, at, :]).then_inc(ld[g], 16)
                            sp.dma_start(ul[:, g, :, :], u_view[:, at, :]).then_inc(ldu[g], 16)
                    turns(sp, QT, turn)

                @block.scalar
                def _(act):
                    def hidden(i, g):
                        act.wait_ge(h1s, i * RING + (g + 1))
                        act.activation(act1[0:2 * D, g, :], ps_h1[0:2 * D, 0:PAIRS * P], ACT.Silu,
                                       bias=b1_col[:, :], scale=1.0).then_inc(si, 1)

                    def turn(i, first):
                        for g in range(RING):
                            if not first:
                                act.wait_ge(put[g], i * (16 * K))
                                act.wait_ge(gt, i * RING + (g + 1 - RING))
                            act.wait_ge(ld[g], i * 16 + 16)
                            act.copy(row_s[:, g, :], src_row[:, bass.ds(i * U + g * K, K)])
                            act.copy(msgs[:, g, :, DEG], recl[:, g, :, R + EW3])
                            act.copy(msgs[:, g, :, MREL], recl[:, g, :, R + SREL]).then_inc(st, 1)
                            if g:
                                hidden(i, g - 1)
                            elif not first:
                                hidden(i - 1, RING - 1)
                            act.wait_ge(tr, i * RING + (g + 1))
                            act.copy(attr_t[:, g, :], ps_at[0:2 * REC, 0:PAIRS * P])
                            act.copy(oht[:, g, :, :].rearrange("p k e -> p (k e)"),
                                     ps_oht[:, :]).then_inc(cp, 1)
                    turns(act, QT, turn)
                    hidden(QT - 1, RING - 1)

                @block.tensor
                def _(pe):
                    def transposes(i, first, g):
                        pe.wait_ge(ohb, i * RING + (g + 1))
                        if g:
                            lone_wait(pe, cp, i * RING + g)
                        elif not first:
                            lone_wait(pe, cp, i * RING)
                        for k in range(K):
                            pe.transpose(ps_oht[:, k * P:(k + 1) * P], oh_b[:, g, k, :], ident_b[:, :])
                        for n in range(PAIRS):
                            m = min(2, K - 2 * n)
                            last = pe.transpose(ps_at[0:m * REC, n * P:(n + 1) * P],
                                                recl[:, g, 2 * n:2 * n + m, :].rearrange("p k f -> p (k f)"),
                                                ident[:, :])
                        last.then_inc(tr, 1)

                    def hidden(i, first, g):
                        pe.wait_ge(cp, i * RING + (g + 1))
                        if g:
                            pe.wait_ge(si, i * RING + g)
                        elif not first:
                            pe.wait_ge(si, i * RING)
                        pe.nop(nofuse=True)
                        pe.matmul(ps_h1[0:2 * D, 0:PAIRS * P], w1t[:, :], attr_t[:, g, :],
                                  start=True, stop=True).then_inc(h1s, 1)

                    def products(i, first, g):
                        ws = windows(PE_ENGINE, win_d, i * U + g * K, K)
                        if g >= 2:
                            lone_wait(pe, v, v_at(i, g - 2, per))
                        elif not first:
                            lone_wait(pe, v, v_at(i - 1, RING - 1 - g, per))
                        for k in range(K):
                            last = pe.matmul(ps_hv[:, g % 2, k * HV:(k + 1) * HV], oht[:, g, k, :],
                                             hv_flat[:, bass.ds(ws[k] * HV, HV)], start=True, stop=True)
                        last.then_inc(hvs, 1)
                        if g:
                            lone_wait(pe, v, v_at(i, g - 1, per))
                        elif not first:
                            lone_wait(pe, v, v_at(i - 1, RING - 1, per))
                        lone_wait(pe, si, i * RING + (g + 1))
                        for n in range(PAIRS):
                            m = min(2, K - 2 * n)
                            last = pe.matmul(ps_gate[:, 2 * n * D:(2 * n + m) * D], act1[:, g, n * P:(n + 1) * P],
                                             w2t[:, 0:m * D], start=True, stop=True)
                        last.then_inc(gt, 1)

                    def turn(i, first):
                        for g in range(RING):
                            before = (i, first, g - 1) if g else None if first else (i - 1, False, RING - 1)
                            if before:
                                hidden(*before)
                            transposes(i, first, g)
                            if before:
                                products(*before)
                    turns(pe, QT, turn)
                    hidden(QT - 1, False, RING - 1)
                    products(QT - 1, False, RING - 1)

                @block.vector
                def _(dve):
                    def bc(a, n):
                        return a.unsqueeze(2).to_broadcast([P, K, n])

                    def finish(i, g):
                        hvg = ps_hv[:, g % 2, 0:K * HV].rearrange("p (k f) -> p k f", k=K)
                        dve.wait_ge(hvs, i * RING + (g + 1))
                        dve.wait_ge(ldu[g], i * 16 + 16)
                        dve.wait_ge(v, v_at(i, g, 0))
                        dve.tensor_tensor(uxv[:, :, :], hvg[:, :, D:D + G], ul[:, g, :, :], ALU.mult)
                        dve.tensor_tensor(scale[:, :], hvg[:, :, D + G], recl[:, g, :, R + CW],
                                          ALU.mult).then_inc(v, 1)
                        dve.wait_ge(v, v_at(i, g, 1))
                        dve.tensor_reduce(logit[:, :], uxv[:, :, :], AX.X, ALU.add).then_inc(v, 1)
                        dve.wait_ge(gt, i * RING + (g + 1))
                        dve.wait_ge(v, v_at(i, g, 2))
                        dve.tensor_tensor(gate_s[:, :, :], ps_gate[:, 0:K * D].rearrange("p (k f) -> p k f", k=K),
                                          bc(logit[:, :], D), ALU.add).then_inc(v, 1)
                        dve.wait_ge(v, v_at(i, g, 3))
                        dve.tensor_tensor(gate_s[:, :, :], gate_s[:, :, :], hvg[:, :, 0:D], ALU.mult).then_inc(v, 1)
                        dve.wait_ge(v, v_at(i, g, 4))
                        dve.tensor_tensor(msgs[:, g, :, 0:D], gate_s[:, :, :], bc(scale[:, :], D),
                                          ALU.mult).then_inc(v, 1)
                        dve.tensor_copy(msgs[:, g, :, TOT], hvg[:, :, D + G]).then_inc(v, 1)

                    def turn(i, first):
                        for g in range(RING):
                            dve.wait_ge(ld[g], i * 16 + 16)
                            if not first:
                                dve.wait_ge(tr, i * RING + (g + 1 - RING))
                            for k in range(K):
                                last = dve.tensor_scalar(oh_b[:, g, k, :], iota_b[:, :],
                                                         recl[:, g, k, R + DREL:R + DREL + 1], None, ALU.is_equal)
                            last.then_inc(ohb, 1)
                            if g >= 2:
                                finish(i, g - 2)
                            elif not first:
                                finish(i - 1, RING - 2 + g)
                    turns(dve, QT, turn)
                    finish(QT - 1, RING - 2)
                    finish(QT - 1, RING - 1)
                    vn[0] = b_v + per * RING * QT

                @block.gpsimd
                def _(pool):
                    last_row = pool.to_reg(SROWS - 1)

                    def turn(i, first):
                        for g in range(RING):
                            lone_wait(pool, st, i * RING + (g + 1))
                            lone_wait(pool, v, v_at(i, g, per))
                            for k in range(K):
                                pool.indirect_dma_start(
                                    msg_dram, bass.IndirectOffsetOnAxis(ap=row_s[:, g, k:k + 1], axis=0),
                                    msgs[:, g, k, :], None, bounds_check=last_row,
                                    oob_is_err=False).then_inc(put[g], 16)
                    turns(pool, QT, turn)
                    for g in range(RING):
                        pool.wait_ge(put[g], QT * 16 * K)
        rows_scope.close()

        with ExitStack() as s5:
            acc = scoped(s5, "acc1", [P, W, AC], F32)
            with ExitStack() as s6:
                ml = scoped(s6, "ml", [P, SR, SB, MSG], F32)
                onehot = scoped(s6, "onehot_src", [P, SR, SB, P], F32)
                sums = s6.enter_context(nc.psum_tensor("sums_src", [P, RING, 512], F32))
                ld = [sem(f"src_load{g}") for g in range(SR)]
                ohs, mm = sem("src_onehot"), sem("src_sum")
                acc_flat = acc[:, :, :].rearrange("p w f -> p (w f)")
                msg_view = msg_dram[0:SROWS, :].rearrange("(n p k) f -> p n (k f)", p=P, k=SB)
                with nc.Block() as block:
                    @block.vector
                    def _(dve):
                        c = chain(dve)
                        c.step(dve.memset(acc_flat, 0.0))
                        keep(c)
                b_v6 = vn[0]

                def v_at6(i, g, k):
                    return i * SR + (b_v6 + g + k)

                with nc.Block() as block:
                    def load_messages(queue, slots):
                        def turn(i, first):
                            for g in slots:
                                if not first:
                                    lone_wait(queue, mm, i * SR + (g + 1 - SR))
                                queue.dma_start(ml[:, g, :, :].rearrange("p k f -> p (k f)"),
                                                msg_view[:, bass.ds(i * SR + g, 1), :].rearrange("p a f -> p (a f)")
                                                ).then_inc(ld[g], 16)
                        turns(queue, ST, turn)

                    @block.sync
                    def _(sp):
                        load_messages(sp, range(0, SR, 2))

                    @block.scalar
                    def _(act):
                        load_messages(act, range(1, SR, 2))

                    @block.vector
                    def _(dve):
                        def finish(i, g, w):
                            dve.wait_ge(mm, i * SR + (g + 1))
                            dve.wait_ge(v, v_at6(i, g, 0))
                            to = acc_flat[:, bass.ds(w * AC, AC)]
                            dve.tensor_tensor(to, to, sums[:, g % RING, 0:AC], ALU.add).then_inc(v, 1)

                        def turn(i, first):
                            for g in range(SR):
                                dve.wait_ge(ld[g], i * 16 + 16)
                                if not first:
                                    dve.wait_ge(mm, i * SR + (g + 1 - SR))
                                for k in range(SB):
                                    last = dve.tensor_scalar(onehot[:, g, k, :], iota[:, :],
                                                             ml[:, g, k, MREL:MREL + 1], None, ALU.is_equal)
                                last.then_inc(ohs, 1)
                                if g == 0:
                                    ws = ([None] * 2 + list(windows(DVE_ENGINE, win_s, 0, RING - 2)) if first
                                          else windows(DVE_ENGINE, win_s, i * SR - 2, RING))
                                elif g == RING:
                                    ws = windows(DVE_ENGINE, win_s, i * SR + (RING - 2), RING)
                                if g >= 2:
                                    finish(i, g - 2, ws[g % RING])
                                elif not first:
                                    finish(i - 1, SR - 2 + g, ws[g])
                        turns(dve, ST, turn)
                        ws = windows(DVE_ENGINE, win_s, SG - 2, 2)
                        for k in range(2):
                            finish(ST - 1, SR - 2 + k, ws[k])
                        vn[0] = b_v6 + SG

                    @block.tensor
                    def _(pe):
                        def turn(i, first):
                            for g in range(SR):
                                pe.wait_ge(ohs, i * SR + (g + 1))
                                if not first or g >= RING:
                                    pe.wait_ge(v, v_at6(i, g - RING, 1))
                                for k in range(SB):
                                    last = pe.matmul(sums[:, g % RING, 0:AC], onehot[:, g, k, :], ml[:, g, k, 0:AC],
                                                     start=(k == 0), stop=(k == SB - 1))
                                last.then_inc(mm, 1)
                        turns(pe, ST, turn)

            square = scoped(s5, "square1", [P, W, D], F32)
            t = scoped(s5, "t1", [P, W, D], F32)

            def row_of(k):
                return rows[:, k, :].unsqueeze(1).to_broadcast([P, W, D])

            def steps(node, c, dve):
                c.step(dve.tensor_scalar(var[:, :], acc[:, :, TOT], 1e-8, None, ALU.max))
                c.step(dve.reciprocal(var[:, :], var[:, :]))
                c.step(dve.tensor_tensor(t[:, :, :], acc[:, :, 0:D], over_features(var[:, :]), ALU.mult))
                c.step(dve.tensor_tensor(t[:, :, :], t[:, :, :], hv[:, :, 0:D], ALU.add))
                node.layernorm(t[:, :, :], t[:, :, :], square[:, :, :], False)
                c.step(dve.tensor_tensor(t[:, :, :], t[:, :, :], row_of(GAMMA), ALU.mult))
                c.step(dve.tensor_tensor(t[:, :, :], t[:, :, :], row_of(BETA), ALU.add))
                c.step(dve.tensor_tensor(X[:, :, :], X[:, :, :], t[:, :, :], ALU.add))
                c.step(dve.tensor_scalar(dis[:, :], acc[:, :, DEG], 1.0, None, ALU.max))
                node.sqrt(dis[:, :])
                c.step(dve.reciprocal(dis[:, :], dis[:, :]))
                c.step(dve.scalar_tensor_tensor(out=dis[:, :], in0=acc[:, :, DEG], scalar=0.0, in1=dis[:, :],
                                                op0=ALU.is_gt, op1=ALU.mult))

            node_block(steps)
        hv_scope.close()

        tab_view = tab_dram.rearrange("(p w) f -> p (w f)", p=P)

        def flat(a):
            return a[:, :, :].rearrange("p w f -> p (w f)")

        acc = sb("acc", [P, W, D])
        ta = sb("ta", [P, W, D])
        tb = sb("tb", [P, W, D])
        third = 1.0 / 3.0

        def steps(node, c, dve):
            node.layernorm(ta[:, :, :], X[:, :, :], tb[:, :, :], True)
            node.store(tab_view, flat(ta))
            c.step(dve.scalar_tensor_tensor(out=X[:, :, :], in0=ta[:, :, :], scalar=third, in1=X[:, :, :],
                                            op0=ALU.mult, op1=ALU.add))
        node_block(steps)
        for layer in range(2):
            propagate(tab_dram, D, EW, acc, False)

            def steps(node, c, dve):
                if layer == 0:
                    node.store(tab_view, flat(acc))
                c.step(dve.scalar_tensor_tensor(out=X[:, :, :], in0=acc[:, :, :], scalar=third, in1=X[:, :, :],
                                                op0=ALU.mult, op1=ALU.add))
            node_block(steps)

        def add_to_x(dve, of, w):
            at = X[:, bass.ds(w, PW), :]
            return dve.tensor_tensor(at, at, of, ALU.add)

        def steps(node, c, dve):
            node.layernorm(ta[:, :, :], X[:, :, :], tb[:, :, :], True)
            c.step(dve.tensor_tensor(tb[:, :, :], ta[:, :, :], over_features(dis[:, :]), ALU.mult))
            node.store(tab_view, flat(tb))
            c.step(dve.tensor_tensor(X[:, :, :], X[:, :, :],
                                     rows[:, BIAS, :].unsqueeze(1).to_broadcast([P, W, D]), ALU.add))
        node_block(steps)
        project(ta, cheb_sb[:, 0, :], add_to_x)
        scaled = sb("scaled", [P, W, D])
        before, term = ta, tb
        for k in range(1, NCHEB):
            propagate(tab_dram, D, EW3, acc, False)
            to = term if k == 1 else before

            def steps(node, c, dve):
                c.step(dve.tensor_tensor(acc[:, :, :], acc[:, :, :], over_features(dis[:, :]), ALU.mult))
                if k == 1:
                    c.step(dve.tensor_scalar(to[:, :, :], acc[:, :, :], -1.0, None, ALU.mult))
                else:
                    c.step(dve.scalar_tensor_tensor(out=to[:, :, :], in0=acc[:, :, :], scalar=-2.0,
                                                    in1=to[:, :, :], op0=ALU.mult, op1=ALU.subtract))
                if k < NCHEB - 1:
                    c.step(dve.tensor_tensor(scaled[:, :, :], to[:, :, :], over_features(dis[:, :]), ALU.mult))
                    node.store(tab_view, flat(scaled))
            node_block(steps)
            project(to, cheb_sb[:, k, :], add_to_x)
            if k > 1:
                before, term = term, before

        with nc.Block() as block:
            @block.sync
            def _(sp):
                s_end = sem("output_stored")
                sp.dma_start(out[0:full].rearrange("(w p) f -> p w f", p=P), X[:, 0:W - 1, :]).then_inc(s_end, 16)
                sp.dma_start(out[full:N], X[0:TAIL, W - 1, :]).then_inc(s_end, 16)
                sp.wait_ge(s_end, 32)


_INS = ["x", "src", "dst", "edge_attr_40", "edge_weight", "node_type_119", "node_vec", "L0_gnn_w", "L0_gnn_b",
        "L1_gnn_W1", "L1_gnn_b1", "L1_gnn_W2", "L1_gnn_b2", "L1_gnn_emb", "L1_gnn_adaptW", "L1_gnn_gamma",
        "L1_gnn_beta", "L3_gnn_weight", "L3_gnn_bias"]


def kernel(**inputs):
    import numpy as _np
    import concourse.bacc as _bacc
    from concourse import mybir as _mybir
    from concourse.bass_utils import run_bass_kernel_spmd as _run

    nc = _bacc.Bacc("TRN2", target_bir_lowering=False, num_devices=1)
    arrays, args = {}, []
    for name in _INS:
        a = _np.ascontiguousarray(inputs[name])
        arrays[f"in_{name}"] = a
        args.append(nc.dram_tensor(f"in_{name}", a.shape, _mybir.dt.from_np(a.dtype), kind="ExternalInput").ap())
    shape = inputs["x"].shape
    args.append(nc.dram_tensor("out_0", shape, _mybir.dt.float32, kind="ExternalOutput").ap())
    gnn_kernel(nc, *args)
    r = _run(nc, [arrays], core_ids=[0])
    return r.results[0]["out_0"]
```
